# Optimizing a Trainium2 kernel written in Bass

```python
import numpy as np
import jax
import jax.numpy as jnp

def _softmax(x, axis=-1):
    return jax.nn.softmax(x, axis=axis)

def _gelu(x):
    return jax.nn.gelu(x, approximate=True)

def _silu(x):
    return jax.nn.silu(x)

def _sigmoid(x):
    return jax.nn.sigmoid(x)

def _layernorm(x, axis=-1, eps=1e-05):
    m = jnp.mean(x, axis=axis, keepdims=True)
    v = jnp.var(x, axis=axis, keepdims=True)
    return (x - m) / jnp.sqrt(v + eps)

def _scatter_add(tgt, idx, src, axis=0):
    return tgt.at[idx].add(src)

def _segment_sum(src, seg, n):
    return jax.ops.segment_sum(src, seg, n)
kernel_name = 'mk_gnn_preln_d2_gnn_r8_72f52d'

def setup_inputs(seed: int=0):
    np.random.seed(seed)
    _w = jnp.asarray

    def _rec_inputs():
        import jax
        import jax.numpy as jnp
        _gk = jax.random.key(seed)
        x = -0.000202 + 1 * jax.random.normal(jax.random.fold_in(_gk, 1), (6250, 128), jnp.float32)
        _s = jax.random.randint(jax.random.fold_in(_gk, 2), (50000,), 0, 6250, jnp.int32)
        _d = jax.random.randint(jax.random.fold_in(_gk, 3), (50000,), 0, 6250, jnp.int32)
        _loop = jnp.arange(6250, dtype=jnp.int32)
        src = jnp.concatenate([_s, _d, _loop])
        dst = jnp.concatenate([_d, _s, _loop])
        _o = jnp.argsort(dst, stable=True)
        src = src[_o]
        dst = dst[_o]
        return (x, src, dst)
    x, src, dst = _rec_inputs()

    def _L0_gnn_setup():
        import jax, jax.numpy as jnp
        import numpy as np
        N_NODES = 6250

        def _sage_conv(x, src, dst, W_l, W_r, b):
            msg = x[src]
            agg = jax.ops.segment_sum(msg, dst, num_segments=N_NODES)
            cnt = jax.ops.segment_sum(jnp.ones_like(dst, dtype=x.dtype), dst, num_segments=N_NODES)
            agg = agg / jnp.maximum(cnt, 1.0)[:, None]
            return agg @ W_l + x @ W_r + b
        key = jax.random.key(seed)
        ks = jax.random.split(key, 8)
        d_in, d_hid, n_edges = (128, 128, 80000)
        s = 1.0 / np.sqrt(d_in)
        return {'x': jax.random.normal(ks[0], (N_NODES, d_in), dtype=jnp.float32), 'edge_index': jax.random.randint(ks[1], (2, n_edges), 0, N_NODES, dtype=jnp.int64), 'W_l0': jax.random.normal(ks[2], (d_in, d_hid), dtype=jnp.float32) * s, 'W_r0': jax.random.normal(ks[3], (d_in, d_hid), dtype=jnp.float32) * s, 'b0': jnp.zeros((d_hid,), dtype=jnp.float32), 'W_l1': jax.random.normal(ks[4], (d_hid, d_hid), dtype=jnp.float32) * s, 'W_r1': jax.random.normal(ks[5], (d_hid, d_hid), dtype=jnp.float32) * s, 'b1': jnp.zeros((d_hid,), dtype=jnp.float32)}
    _L0_gnn_all = _L0_gnn_setup()
    _L0_gnn_in = {k: v for k, v in _L0_gnn_all.items() if k in ('W_l0', 'W_r0', 'b0', 'W_l1', 'W_r1', 'b1')}
    del _L0_gnn_all

    def _L1_gnn_setup():
        import jax, jax.numpy as jnp
        import numpy as np
        import math
        N = 6250
        E = 100000
        H = 128
        AVG_DEGREE = 16
        key = jax.random.key(seed)
        ks = jax.random.split(key, 6)
        x = jax.random.normal(ks[0], (N, H), dtype=jnp.float32)
        edge_index = jax.random.randint(ks[1], (2, E), 0, N, dtype=jnp.int64)
        W_interact = jax.random.normal(ks[2], (2 * H, H), dtype=jnp.float32) / np.sqrt(2 * H)
        b_interact = jnp.zeros((H,), dtype=jnp.float32)
        W_update = jax.random.normal(ks[3], (H, H), dtype=jnp.float32) / np.sqrt(H)
        b_update = jnp.zeros((H,), dtype=jnp.float32)
        return {'x': x, 'edge_index': edge_index, 'W_interact': W_interact, 'b_interact': b_interact, 'W_update': W_update, 'b_update': b_update}
    _L1_gnn_all = _L1_gnn_setup()
    _L1_gnn_in = {k: v for k, v in _L1_gnn_all.items() if k in ('W_interact', 'b_interact', 'W_update', 'b_update')}
    del _L1_gnn_all
    return {'x': x, 'src': src, 'dst': dst, 'L0_gnn_W_l0': _L0_gnn_in['W_l0'], 'L0_gnn_W_r0': _L0_gnn_in['W_r0'], 'L0_gnn_b0': _L0_gnn_in['b0'], 'L0_gnn_W_l1': _L0_gnn_in['W_l1'], 'L0_gnn_W_r1': _L0_gnn_in['W_r1'], 'L0_gnn_b1': _L0_gnn_in['b1'], 'L1_gnn_W_interact': _L1_gnn_in['W_interact'], 'L1_gnn_b_interact': _L1_gnn_in['b_interact'], 'L1_gnn_W_update': _L1_gnn_in['W_update'], 'L1_gnn_b_update': _L1_gnn_in['b_update']}

def reference(x, src, dst, L0_gnn_W_l0, L0_gnn_W_r0, L0_gnn_b0, L0_gnn_W_l1, L0_gnn_W_r1, L0_gnn_b1, L1_gnn_W_interact, L1_gnn_b_interact, L1_gnn_W_update, L1_gnn_b_update):
    import jax
    import jax.numpy as jnp

    def _L0_gnn_ref(x, edge_index, W_l0, W_r0, b0, W_l1, W_r1, b1):
        import jax, jax.numpy as jnp
        import numpy as np
        N_NODES = 6250

        def _sage_conv(x, src, dst, W_l, W_r, b):
            msg = x[src]
            agg = jax.ops.segment_sum(msg, dst, num_segments=N_NODES)
            cnt = jax.ops.segment_sum(jnp.ones_like(dst, dtype=x.dtype), dst, num_segments=N_NODES)
            agg = agg / jnp.maximum(cnt, 1.0)[:, None]
            return agg @ W_l + x @ W_r + b
        src, dst = (edge_index[0], edge_index[1])
        h = jax.nn.relu(_sage_conv(x, src, dst, W_l0, W_r0, b0))
        h = jax.nn.relu(_sage_conv(h, src, dst, W_l1, W_r1, b1))
        return h

    def _L1_gnn_ref(x, edge_index, W_interact, b_interact, W_update, b_update):
        import jax, jax.numpy as jnp
        import numpy as np
        import math
        N = 6250
        E = 100000
        H = 128
        AVG_DEGREE = 16
        src, dst = (edge_index[0], edge_index[1])
        h_edge = jnp.concatenate([x[src], x[dst]], axis=-1)
        m_ij = jax.nn.relu(h_edge @ W_interact + b_interact)
        m_i = jax.ops.segment_sum(m_ij, src, num_segments=x.shape[0])
        m_i = m_i / jnp.asarray(math.sqrt(AVG_DEGREE), dtype=x.dtype)
        out = x + jax.nn.relu((x + m_i) @ W_update + b_update)
        return out
    edge_index = jnp.stack([src, dst])
    h = jnp.maximum(_layernorm(x, axis=-1), 0.0)
    x = x + _L0_gnn_ref(h, edge_index, L0_gnn_W_l0, L0_gnn_W_r0, L0_gnn_b0, L0_gnn_W_l1, L0_gnn_W_r1, L0_gnn_b1)
    h = jnp.maximum(_layernorm(x, axis=-1), 0.0)
    x = x + _L1_gnn_ref(h, edge_index, L1_gnn_W_interact, L1_gnn_b_interact, L1_gnn_W_update, L1_gnn_b_update)
    return x

_drawn_inputs = setup_inputs


def setup_inputs(seed=0):
    import zlib

    import numpy as np

    out = dict(_drawn_inputs(seed))
    spreads = {'L0_gnn_b0': (0.0, 0.1),
     'L0_gnn_b1': (0.0, 0.1),
     'L1_gnn_b_interact': (0.0, 0.1),
     'L1_gnn_b_update': (0.0, 0.323)}
    factors = {}
    for name, (base, spread) in spreads.items():
        noise = np.random.default_rng([zlib.crc32(name.encode()), seed]).standard_normal(out[name].shape)
        drawn = base * np.exp(spread * noise) if base else spread * noise
        out[name] = jnp.asarray(drawn.astype(out[name].dtype))
    for name, factor in factors.items():
        out[name] = (out[name] * factor).astype(out[name].dtype)
    return out
```

```python
import concourse.bass as bass
from concourse import mybir
from contextlib import ExitStack



def gnn_kernel(nc, x, src, dst, W_l0, W_r0, b0, W_l1, W_r1, b1, W_int, b_int, W_upd, b_upd, out):
    f32 = mybir.dt.float32
    i32 = mybir.dt.int32
    ALU = mybir.AluOpType
    ACT = mybir.ActivationFunctionType
    AX = mybir.AxisListType
    P = 128
    N, D = x.shape
    E = src.shape[0]
    EPS = 1e-05
    J = 4
    GE = J * P
    NG = -(-E // GE)
    HG = NG // 2
    WIN = 64
    TRASH = -(-N // P) * P
    ROWS = TRASH + P
    NT = ROWS // P
    CT = 5
    CW = CT * P
    NC = NT // CT
    HALF = CW // 2
    MAXR = -(-(N + 1) // WIN)
    FILLS = 16 * NC
    S1 = 4
    assert NG == 2 * HG and NG % S1 == 0 and HG <= P and NT == CT * NC and NC % 2 == 0
    assert TRASH + WIN <= ROWS and NC >= 4
    PAD = N

    ctx = ExitStack()
    with ctx:
        def sb(name, shape, dt=f32):
            return ctx.enter_context(nc.sbuf_tensor(name, shape, dt))

        def sem(name):
            return ctx.enter_context(nc.semaphore(name))

        def dram(name, shape):
            return nc.dram_tensor(name, shape, f32).ap()

        h0_rows = dram("h0_rows", [ROWS, D])
        h1_rows = dram("h1_rows", [ROWS, D])
        a_rows = dram("a_rows", [ROWS, D])
        b_rows = dram("b_rows", [ROWS, D])
        acc = [dram(f"acc{c}", [ROWS, D]) for c in range(2)]

        x_sb = sb("x_sb", [P, NT, D])
        hT = sb("hT", [P, ROWS])
        h3 = hT[:, :].rearrange("p (t f) -> p t f", f=D)
        agg = sb("agg", [P, 2, ROWS])
        src_r = sb("src_r", [HG, 2, GE], i32)
        dst_r = sb("dst_r", [HG, 2, GE], i32)
        src_rf = sb("src_rf", [HG, 2, GE])
        dst_rf = sb("dst_rf", [HG, 2, GE])
        gmin = sb("gmin", [HG, 2])
        gspan = sb("gspan", [HG, 2])
        diag = sb("diag", [HG, 4, HG])
        src_f = sb("src_f", [P, NG, J])
        src_i = sb("src_i", [P, NG, J], i32)
        dst_f = sb("dst_f", [P, NG, J])
        rel_f = sb("rel_f", [P, NG, J])
        base_f = sb("base_f", [P, NG])
        base_w = sb("base_w", [1, NG])
        base_i = sb("base_i", [1, NG], i32)
        span = sb("span", [1, 1])
        thr = sb("thr", [1, MAXR])
        rounds_f = sb("rounds_f", [1, 1])
        rounds_i = sb("rounds_i", [1, 1], i32)
        ident = sb("ident", [P, P])
        ones = sb("ones", [P, P])
        tri = sb("tri", [P, P])
        iota_w = sb("iota_w", [P, WIN])
        trash_p = sb("trash_p", [P, 1])
        zeros = sb("zeros", [P, CT, D])
        wl = [sb("wl0", [P, D]), sb("wl1", [P, D])]
        wr = [sb("wr0", [P, D]), sb("wr1", [P, D])]
        bc = [sb("bc0", [P, 1]), sb("bc1", [P, 1])]
        w_ab = sb("w_ab", [P, 2 * D])
        w_u = sb("w_u", [P, D])
        brow = sb("brow", [1, 3, D])
        stats = sb("stats", [P, NT, 6])
        lnw = sb("lnw", [P, 10, NT])
        idx1 = sb("idx1", [P, S1, J], i32)
        onehot = sb("onehot", [P, S1, J, WIN])
        rows_g = sb("rows_g", [P, S1, J, D])
        hrow = sb("hrow", [P, 2, CT, D])
        mslot = sb("mslot", [P, 2, CW])
        tslot = sb("tslot", [P, 2, CW])
        abslot = sb("abslot", [P, 2, CT, 2 * D])
        src_s = sb("src_s", [P, 2, J])
        eq = sb("eq", [P, 2, J, P])
        eqt = sb("eqt", [P, J, P])
        dupe = sb("dupe", [P, 4, J])
        mask = sb("mask", [P, 2, J])
        sidx = sb("sidx", [P, 2, J], i32)
        ohT = sb("ohT", [WIN, 2, GE])
        bwin = sb("bwin", [WIN, 2, D])
        msum = sb("msum", [P, 2, J, D])
        msg = sb("msg", [P, 2, J, D])
        val = sb("val", [P, 2, J, D])
        y_sb = rows_g[:, :, :, :].rearrange("p s j f -> p (s j) f")

        ps = ctx.enter_context(nc.psum_tensor("ps", [P, 8, 512], f32))
        ps_f = ps[:, :, :].rearrange("p b n -> p (b n)")

        s_pads = sem("s_pads")
        s_const = sem("s_const")
        s_edges = sem("s_edges")
        s_x = sem("s_x")
        s_w = sem("s_w")
        s_diag = sem("s_diag")
        s_et = sem("s_et")
        s_dve = sem("s_dve")
        s_rounds = sem("s_rounds")

        def norm_sems(k):
            return {n: sem(f"s_{n}_{k}") for n in (
                "bnst", "var", "sqrt", "ln", "hrows", "hT_ps", "hT_ok", "t_ok", "ab_ps", "ab_ok")} | {
                "st": [sem(f"s_st_{k}_{s}") for s in range(2)]}

        def agg_sems(k):
            return {n: sem(f"s_{n}_{k}") for n in (
                "window", "idx", "onehot", "issue", "psum", "added", "done", "shift")} | {
                "gathered": [sem(f"s_gathered_{k}_{s}") for s in range(S1)]}

        def lin_sems(k):
            return {n: sem(f"s_{n}_{k}") for n in (
                "mean", "lin", "relu", "kept", "tr", "rows")} | {
                "st": [sem(f"s_lst_{k}_{s}") for s in range(2)]}

        NS = [norm_sems(0), norm_sems(1)]
        AS = [agg_sems(0), agg_sems(1)]
        LS = [lin_sems(0), lin_sems(1)]
        s_rcnt = sem("s_rcnt")
        e_window = sem("e_window")
        e_shift = sem("e_shift")
        e_loads = sem("e_loads")
        e_idx = sem("e_idx")
        e_onehot = sem("e_onehot")
        e_issue = sem("e_issue")
        e_gathered = [sem(f"e_gathered{s}") for s in range(2)]
        e_bwin = [sem(f"e_bwin{s}") for s in range(2)]
        e_spread = sem("e_spread")
        e_ohT = sem("e_ohT")
        e_bm = sem("e_bm")
        e_eq = sem("e_eq")
        e_small = sem("e_small")
        e_sidx = sem("e_sidx")
        e_msum = sem("e_msum")
        e_msg = sem("e_msg")
        e_presum = sem("e_presum")
        e_val = sem("e_val")
        e_turn = sem("e_turn")
        e_scattered = [sem(f"e_scattered{c}") for c in range(2)]
        o_acc = [sem(f"o_acc{s}") for s in range(2)]
        o_y1 = sem("o_y1")
        o_y = sem("o_y")
        o_tr = sem("o_tr")
        o_t = sem("o_t")
        o_lin = sem("o_lin")
        o_relu = sem("o_relu")
        o_x = sem("o_x")
        o_sum = sem("o_sum")
        o_st = [sem(f"o_st{s}") for s in range(2)]

        block = ctx.enter_context(nc.Block())

        def chunk_rows(table, c):
            return table[bass.ds(c * CW, CW), :].rearrange("(t p) f -> p t f", p=P)

        FULL = (N // P) * P
        LAST = N - FULL
        G1 = (E - HG * GE) // GE
        TAIL = E - (HG + G1) * GE

        @block.sync
        def _(sp):
            sp.wait_ge(s_pads, 5)
            for to, of in ((dst_r, dst), (src_r, src)):
                sp.dma_start(to[:, 0, :], of[0:HG * GE].rearrange("(q e) -> q e", e=GE)).then_inc(s_edges, 16)
                sp.dma_start(to[0:G1, 1, :], of[HG * GE:(HG + G1) * GE].rearrange("(q e) -> q e", e=GE)
                             ).then_inc(s_edges, 16)
                sp.dma_start(to[G1:G1 + 1, 1, 0:TAIL], of[(HG + G1) * GE:E].rearrange("(a e) -> a e", a=1)
                             ).then_inc(s_edges, 16)
            for w, of in ((wl[0], W_l0), (wr[0], W_r0), (wl[1], W_l1), (wr[1], W_r1), (w_u, W_upd)):
                sp.dma_start(w[:, :], of).then_inc(s_w, 16)
            for h in range(2):
                sp.dma_start(w_ab[:, h * D:(h + 1) * D], W_int[h * D:(h + 1) * D, :]).then_inc(s_w, 16)
            sp.dma_start(brow[:, 1, :], b_int.rearrange("(a n) -> a n", a=1)).then_inc(s_w, 16)
            sp.dma_start(brow[:, 2, :], b_upd.rearrange("(a n) -> a n", a=1)).then_inc(s_w, 16)
            sp.dma_start(bc[0][:, :], b0.rearrange("(n a) -> n a", a=1)).then_inc(s_w, 16)
            sp.dma_start(bc[1][:, :], b1.rearrange("(n a) -> n a", a=1)).then_inc(s_w, 16)

            def store_h0(c, s):
                sp.wait_ge(NS[0]["hrows"], c + 1)
                sp.dma_start(chunk_rows(h0_rows, c), hrow[:, s, :, :]).then_inc(NS[0]["st"][s], 16)

            with sp.Fori(0, NC // 2) as u:
                for s in range(2):
                    store_h0(2 * u + s, s)

            def store_h1(c, s):
                sp.wait_ge(LS[0]["rows"], c + 1)
                sp.dma_start(chunk_rows(h1_rows, c), hrow[:, s, :, :]).then_inc(LS[0]["st"][s], 16)

            with sp.Fori(0, NC // 2) as u:
                for s in range(2):
                    store_h1(2 * u + s, s)

            def store_ab(c, s):
                sp.wait_ge(NS[1]["ab_ok"], c + 1)
                sp.dma_start(chunk_rows(a_rows, c), abslot[:, s, :, 0:D]).then_inc(NS[1]["st"][s], 16)
                sp.dma_start(chunk_rows(b_rows, c), abslot[:, s, :, D:2 * D]).then_inc(NS[1]["st"][s], 16)

            with sp.Fori(0, NC // 2) as u:
                for s in range(2):
                    store_ab(2 * u + s, s)
            for s in range(2):
                sp.wait_ge(NS[1]["st"][s], 32 * NC // 2)

            sp.wait_ge(s_rounds, 1)
            rounds = sp.value_load(rounds_i[0:1, 0:1], min_val=1, max_val=MAXR)
            with sp.Fori(0, rounds) as r:
                sp.wait_ge(e_window, r + 1)
                sp.sem_inc(e_loads, 1)
                with sp.Fori(0, NG // 2) as u:
                    for s in range(2):
                        base = sp.value_load(base_i[0:1, bass.ds(2 * u + s, 1)], min_val=0, max_val=ROWS - WIN)
                        sp.wait_ge(e_bm, r * NG + 2 * u + s + 1)
                        sp.dma_start(bwin[:, s, :], b_rows[bass.ds(base, WIN), :]).then_inc(e_bwin[s], 16)

            for c in range(2):
                sp.wait_ge(e_scattered[c], 32 * NG * rounds + FILLS)
                sp.sem_inc(e_loads, 1)

            def load_acc(c, s):
                sp.dma_start(hrow[:, s, :, :], chunk_rows(acc[0], c)).then_inc(o_acc[s], 16)
                sp.dma_start(mslot[:, s, :].rearrange("p (t f) -> p t f", f=D), chunk_rows(acc[1], c)
                             ).then_inc(o_acc[s], 16)

            def store_out(c, s):
                sp.wait_ge(o_sum, c + 1)
                sp.dma_start(chunk_rows(out, c), abslot[:, s, :, 0:D]).then_inc(o_st[s], 16)

            load_acc(0, 0)
            load_acc(1, 1)
            with sp.Fori(0, NC // 2 - 1) as u:
                for s in range(2):
                    store_out(2 * u + s, s)
                    load_acc(2 * u + 2 + s, s)
            store_out(NC - 2, 0)
            done = (NC - 1) * CW
            sp.wait_ge(o_sum, NC)
            sp.dma_start(out[done:FULL, :].rearrange("(t p) f -> p t f", p=P),
                         abslot[:, 1, 0:(FULL - done) // P, 0:D]).then_inc(o_st[1], 16)
            sp.dma_start(out[FULL:N, :], abslot[0:LAST, 1, (FULL - done) // P, 0:D]).then_inc(o_st[1], 16)
            sp.wait_ge(o_st[0], 16 * (NC // 2))
            sp.wait_ge(o_st[1], 16 * (NC // 2) + 16)

        @block.gpsimd
        def _(pool):
            nc.gpsimd.memset(src_r[:, 1, :], PAD).then_inc(s_pads, 1)
            nc.gpsimd.memset(dst_r[:, 1, :], PAD).then_inc(s_pads, 1)
            nc.gpsimd.memset(x_sb[:, NT - 2:NT, :], 0.0).then_inc(s_pads, 1)
            nc.gpsimd.memset(zeros[:, :, :], 0.0).then_inc(s_pads, 1)
            nc.gpsimd.memset(brow[:, 0, :], 0.0).then_inc(s_pads, 1)
            nc.gpsimd.memset(ident[:, :], 0.0).then_inc(s_const, 1)
            nc.gpsimd.memset(ones[:, :], 1.0).then_inc(s_const, 1)
            nc.gpsimd.memset(tri[:, :], 1.0).then_inc(s_const, 1)
            nc.gpsimd.iota(iota_w[:, :], pattern=[[1, WIN]], base=0, channel_multiplier=0,
                           allow_small_or_imprecise_dtypes=True).then_inc(s_const, 1)
            nc.gpsimd.iota(trash_p[:, :], pattern=[[0, 1]], base=TRASH, channel_multiplier=1,
                           allow_small_or_imprecise_dtypes=True).then_inc(s_const, 1)
            nc.gpsimd.iota(thr[:, :], pattern=[[WIN, MAXR]], base=WIN, channel_multiplier=0,
                           allow_small_or_imprecise_dtypes=True).then_inc(s_const, 1)
            pool.wait_ge(s_const, 6)
            nc.gpsimd.affine_select(out=ident[:, :], in_=ident[:, :], compare_op=ALU.not_equal, fill=1.0,
                                    base=0, pattern=[[-1, P]], channel_multiplier=1).then_inc(s_const, 1)
            nc.gpsimd.affine_select(out=tri[:, :], in_=tri[:, :], compare_op=ALU.is_gt, fill=0.0,
                                    base=0, pattern=[[-1, P]], channel_multiplier=1).then_inc(s_const, 1)
            pool.wait_ge(s_pads, 5)
            for c in range(2):
                for k in range(NC):
                    pool.dma_start(acc[c][k * CW:(k + 1) * CW, :].rearrange("(t p) f -> p t f", p=P),
                                   zeros[:, :, :]).then_inc(e_scattered[c], 16)
            pool.wait_ge(s_rounds, 1)
            rounds = pool.value_load(rounds_i[0:1, 0:1], min_val=1, max_val=MAXR)

            def aggregate(A, table):
                with pool.Fori(0, rounds) as r:
                    with pool.Fori(0, NG // S1) as u:
                        for s in range(S1):
                            pool.wait_ge(A["idx"], r * NG + S1 * u + s + 1)
                            pool.sem_inc(A["issue"], 1)
                            for j in range(J):
                                nc.gpsimd.indirect_dma_start(
                                    rows_g[:, s, j, :], None, table,
                                    bass.IndirectOffsetOnAxis(ap=idx1[:, s, j:j + 1], axis=0)
                                ).then_inc(A["gathered"][s], 16)

            for s in range(2):
                pool.wait_ge(NS[0]["st"][s], 16 * NC // 2)
            aggregate(AS[0], h0_rows)
            for s in range(2):
                pool.wait_ge(LS[0]["st"][s], 16 * NC // 2)
            aggregate(AS[1], h1_rows)

            for s in range(2):
                pool.wait_ge(NS[1]["st"][s], 32 * NC // 2)
            pool.sem_inc(e_turn, 1)

            def gather(r, g, s):
                pool.wait_ge(e_idx, r * NG + g + 1)
                pool.sem_inc(e_issue, 1)
                for j in range(J):
                    nc.gpsimd.indirect_dma_start(
                        rows_g[:, s, j, :], None, a_rows,
                        bass.IndirectOffsetOnAxis(ap=idx1[:, s, j:j + 1], axis=0)
                    ).then_inc(e_gathered[s], 16)

            def scatter(r, g, s):
                pool.wait_ge(e_sidx, r * NG + g + 1)
                pool.wait_ge(e_val, r * NG + g + 1)
                for j in range(J):
                    pool.wait_ge(e_scattered[j % 2], (r * NG + g) * 32 + 16 * (j // 2) + FILLS)
                    pool.sem_inc(e_turn if j == 1 else e_issue, 1)
                    nc.gpsimd.indirect_dma_start(
                        acc[j % 2], bass.IndirectOffsetOnAxis(ap=sidx[:, s, j:j + 1], axis=0),
                        val[:, s, j, :], None, compute_op=ALU.add).then_inc(e_scattered[j % 2], 16)

            with pool.Fori(0, rounds) as r:
                for s in range(2):
                    gather(r, s, s)
                with pool.Fori(0, NG // 2 - 1) as u:
                    for s in range(2):
                        scatter(r, 2 * u + s, s)
                        gather(r, 2 * u + 2 + s, s)
                for s in range(2):
                    scatter(r, NG - 2 + s, s)

        @block.scalar
        def _(act):
            act.wait_ge(s_pads, 5)
            act.dma_start(x_sb[:, 0:N // P, :], x[0:FULL, :].rearrange("(t p) f -> p t f", p=P)).then_inc(s_x, 16)
            act.dma_start(x_sb[0:LAST, N // P, :], x[FULL:N, :]).then_inc(s_x, 16)

            def norm_scale(S):
                act.wait_ge(S["var"], 1)
                nc.scalar.activation(lnw[:, 4, :], lnw[:, 3, :], ACT.Sqrt).then_inc(S["sqrt"], 1)
                act.wait_ge(S["ln"], 1)

            def norm_rows(S, c, s):
                for k in range(CT):
                    t = c * CT + k
                    last = nc.scalar.activation(
                        hrow[:, s, k, :], x_sb[:, bass.ds(t, 1), :].rearrange("p a f -> p (a f)"), ACT.Relu,
                        bias=lnw[:, 6, bass.ds(t, 1)], scale=lnw[:, 5, bass.ds(t, 1)])
                last.then_inc(S["hrows"], 1)

            norm_scale(NS[0])
            for s in range(2):
                norm_rows(NS[0], s, s)
            with act.Fori(1, NC // 2) as u:
                for s in range(2):
                    act.wait_ge(NS[0]["st"][s], 16 * u)
                    act.wait_ge(NS[0]["hT_ps"], 2 * u + s - 1)
                    norm_rows(NS[0], 2 * u + s, s)

            def linear(L, c, s):
                act.wait_ge(LS[L]["lin"], c + 1)
                nc.scalar.activation(tslot[:, s, :].rearrange("p (h n) -> p h n", h=2),
                                     ps[:, 4 * s:4 * s + 2, 0:HALF], ACT.Relu,
                                     bias=bc[L][:, 0:1]).then_inc(LS[L]["relu"], 1)

            act.wait_ge(s_w, 16 * 11)
            for L in range(2):
                for s in range(2):
                    linear(L, s, s)
                with act.Fori(1, NC // 2) as u:
                    for s in range(2):
                        act.wait_ge(LS[L]["tr"], 2 * u + s - 1)
                        if L == 0:
                            act.wait_ge(LS[L]["kept"], 2 * u + s - 1)
                        linear(L, 2 * u + s, s)

            norm_scale(NS[1])

            def store_ab(c, s):
                act.wait_ge(NS[1]["ab_ps"], c + 1)
                nc.scalar.activation(abslot[:, s, :, :].rearrange("p t n -> p (t n)"), ps_f[:, 2048:2048 + CT * 2 * D],
                                     ACT.Copy).then_inc(NS[1]["ab_ok"], 1)

            for s in range(2):
                norm_rows(NS[1], s, s)
                store_ab(s, s)
            with act.Fori(1, NC // 2) as u:
                for s in range(2):
                    act.wait_ge(NS[1]["hT_ok"], 4 * u + 2 * s - 2)
                    norm_rows(NS[1], 2 * u + s, s)
                    act.wait_ge(NS[1]["st"][s], 32 * u)
                    store_ab(2 * u + s, s)

            act.wait_ge(s_rounds, 1)
            rounds = act.value_load(rounds_i[0:1, 0:1], min_val=1, max_val=MAXR)
            with act.Fori(0, rounds) as r:
                with act.Fori(0, NG // 2) as u:
                    for s in range(2):
                        it = r * NG + 2 * u + s
                        act.wait_ge(e_spread, it + 1)
                        nc.scalar.activation(ohT[:, s, :], ps[0:WIN, 4 * s + 1, :], ACT.Copy).then_inc(e_ohT, 1)
                        act.wait_ge(e_msum, it + 1)
                        for j in range(J):
                            last = nc.scalar.activation(msg[:, s, j, :], msum[:, s, j, :], ACT.Relu,
                                                        scale=mask[:, s, j:j + 1])
                        last.then_inc(e_msg, 1)
                        act.wait_ge(e_presum, it + 1)
                        act.wait_ge(e_turn, it + 1)
                        nc.scalar.activation(val[:, s, :, :].rearrange("p j f -> p (j f)"), ps[:, 4 * s + 3, :],
                                             ACT.Copy).then_inc(e_val, 1)

            def out_steps(c, s):
                act.wait_ge(o_tr, c + 1)
                nc.scalar.activation(tslot[:, s, :], ps_f[:, 2048 * s:2048 * s + CW], ACT.Copy).then_inc(o_t, 1)
                act.wait_ge(o_lin, c + 1)
                nc.scalar.activation(abslot[:, s, :, D:2 * D],
                                     ps_f[:, 2048 * s + 1024:2048 * s + 1024 + CW].rearrange("p (t f) -> p t f", f=D),
                                     ACT.Relu).then_inc(o_relu, 1)

            for s in range(2):
                out_steps(s, s)
            with act.Fori(1, NC // 2) as u:
                for s in range(2):
                    act.wait_ge(o_sum, 2 * u + s - 1)
                    out_steps(2 * u + s, s)

        @block.tensor
        def _(pe):
            pe.wait_ge(s_const, 8)
            pe.wait_ge(s_diag, 4)
            for h in range(2):
                for a, rows in enumerate((dst_rf, src_rf)):
                    for j in range(J):
                        nc.tensor.transpose(ps[:, 2 * h + a, j * HG:(j + 1) * HG], rows[:, h, j * P:(j + 1) * P],
                                            ident[0:HG, 0:HG])
            for k in range(4):
                last = nc.tensor.matmul(ps[:, 4 + k // 2, (k % 2) * HG:(k % 2 + 1) * HG], ones[0:HG, :],
                                        diag[:, k, :], start=True, stop=True)
            last.then_inc(s_et, 1)

            def norm_transpose(S, c, s):
                pe.wait_ge(S["hrows"], c + 1)
                for k in range(CT):
                    last = nc.tensor.transpose(ps_f[:, 1024 * s + k * P:1024 * s + (k + 1) * P], hrow[:, s, k, :],
                                               ident[:, :])
                last.then_inc(S["hT_ps"], 1)

            pe.wait_ge(s_rounds, 1)
            for s in range(2):
                norm_transpose(NS[0], s, s)
            with pe.Fori(1, NC // 2) as u:
                for s in range(2):
                    pe.wait_ge(NS[0]["hT_ok"], 2 * u + s - 1)
                    norm_transpose(NS[0], 2 * u + s, s)

            rounds = pe.value_load(rounds_i[0:1, 0:1], min_val=1, max_val=MAXR)
            pe.wait_ge(NS[0]["hT_ok"], NC)
            pe.wait_ge(s_w, 16 * 11)

            for L in range(2):
                A = AS[L]
                with pe.Fori(0, rounds) as r:
                    with pe.Fori(0, NG // S1) as u:
                        for s in range(S1):
                            pe.wait_ge(A["onehot"], r * NG + S1 * u + s + 1)
                            pe.wait_ge(A["gathered"][s], 16 * J * (r * (NG // S1) + u + 1))
                            for j in range(J):
                                last = nc.tensor.matmul(ps[:, s, 0:WIN], rows_g[:, s, j, :], onehot[:, s, j, :],
                                                        start=j == 0, stop=j == J - 1)
                            if L == 0:
                                for j in range(J):
                                    last = nc.tensor.matmul(ps[:, s, WIN:2 * WIN], ones[:, :], onehot[:, s, j, :],
                                                            start=j == 0, stop=j == J - 1)
                            last.then_inc(A["psum"], 1)
                pe.wait_ge(A["done"], 1)

                def linear(c, s):
                    pe.wait_ge(LS[L]["mean"], c + 1)
                    for h in range(2):
                        nc.tensor.matmul(ps[:, 4 * s + h, 0:HALF], wl[L][:, :], mslot[:, s, h * HALF:(h + 1) * HALF],
                                         start=True, stop=False)
                        last = nc.tensor.matmul(ps[:, 4 * s + h, 0:HALF], wr[L][:, :],
                                                hT[:, bass.ds(c * CW + h * HALF, HALF)], start=False, stop=True)
                    last.then_inc(LS[L]["lin"], 1)
                    pe.wait_ge(LS[L]["relu"], c + 1)
                    for k in range(CT):
                        last = nc.tensor.transpose(ps_f[:, 2048 * s + 1024 + k * P:2048 * s + 1024 + (k + 1) * P],
                                                   tslot[:, s, k * P:(k + 1) * P], ident[:, :])
                    last.then_inc(LS[L]["tr"], 1)

                for s in range(2):
                    linear(s, s)
                with pe.Fori(1, NC // 2) as u:
                    for s in range(2):
                        pe.wait_ge(LS[L]["rows"], 2 * u + s - 1)
                        linear(2 * u + s, s)

            def ab_step(c, s):
                norm_transpose(NS[1], c, s)
                pe.wait_ge(NS[1]["t_ok"], c + 1)
                for k in range(CT):
                    o = 2048 + k * 2 * D
                    nc.tensor.matmul(ps_f[:, o:o + 2 * D], tslot[:, s, k * P:(k + 1) * P], w_ab[:, :],
                                     start=True, stop=False)
                    last = nc.tensor.matmul(ps_f[:, o:o + 2 * D], ones[0:1, :],
                                            brow[:, 0:2, :].rearrange("p a n -> p (a n)"), start=False, stop=True)
                last.then_inc(NS[1]["ab_ps"], 1)

            ab_step(0, 0)
            pe.wait_ge(NS[1]["ab_ok"], 1)
            ab_step(1, 1)
            with pe.Fori(1, NC // 2) as u:
                for s in range(2):
                    pe.wait_ge(NS[1]["ab_ok"], 2 * u + s)
                    ab_step(2 * u + s, s)
            pe.wait_ge(NS[1]["ab_ok"], NC)

            pe.sem_inc(e_bm, 2)
            with pe.Fori(0, rounds) as r:
                with pe.Fori(0, NG // 2) as u:
                    for s in range(2):
                        it = r * NG + 2 * u + s
                        pe.wait_ge(e_onehot, it + 1)
                        for j in range(J):
                            nc.tensor.matmul(ps[:, 4 * s, j * P:(j + 1) * P],
                                             src_s[:, s, j:j + 1].to_broadcast([P, P]), ident[:, :],
                                             start=True, stop=True)
                        for j in range(J):
                            last = nc.tensor.transpose(ps[0:WIN, 4 * s + 1, j * P:(j + 1) * P], onehot[:, s, j, :],
                                                       ident[:, :])
                        last.then_inc(e_spread, 1)
                        pe.wait_ge(e_ohT, it + 1)
                        pe.wait_ge(e_bwin[s], 16 * (r * (NG // 2) + u + 1))
                        for j in range(J):
                            last = nc.tensor.matmul(ps[:, 4 * s + 2, j * D:(j + 1) * D],
                                                    ohT[:, s, j * P:(j + 1) * P], bwin[:, s, :], start=True, stop=True)
                        last.then_inc(e_bm, 1)
                        pe.wait_ge(e_eq, it + 1)
                        pe.wait_ge(e_msg, it + 1)
                        for j in range(J):
                            last = nc.tensor.matmul(ps[:, 4 * s + 3, j * D:(j + 1) * D], eq[:, s, j, :],
                                                    msg[:, s, j, :], start=True, stop=True)
                        last.then_inc(e_presum, 1)
            pe.wait_ge(e_val, NG * rounds)

            def out_steps(c, s):
                pe.wait_ge(o_y, c + 1)
                for k in range(CT):
                    last = nc.tensor.transpose(ps_f[:, 2048 * s + k * P:2048 * s + (k + 1) * P], y_sb[:, s * CT + k, :],
                                               ident[:, :])
                last.then_inc(o_tr, 1)
                pe.wait_ge(o_t, c + 1)
                for k in range(CT):
                    o = 2048 * s + 1024 + k * P
                    nc.tensor.matmul(ps_f[:, o:o + P], tslot[:, s, k * P:(k + 1) * P], w_u[:, :],
                                     start=True, stop=False)
                    last = nc.tensor.matmul(ps_f[:, o:o + P], ones[0:1, :], brow[:, 2, :], start=False, stop=True)
                last.then_inc(o_lin, 1)

            for s in range(2):
                out_steps(s, s)
            with pe.Fori(1, NC // 2) as u:
                for s in range(2):
                    pe.wait_ge(o_relu, 2 * u + s - 1)
                    out_steps(2 * u + s, s)

        @block.vector
        def _(dve):
            steps = [0]

            def link(instruction):
                steps[0] += 1
                instruction.then_inc(s_dve, 1)
                dve.wait_ge(s_dve, steps[0])

            v = nc.vector
            dve.wait_ge(s_edges, 16 * 6)
            dve.wait_ge(s_const, 8)
            v.tensor_copy(dst_rf[:, :, :], dst_r[:, :, :])
            link(v.tensor_copy(src_rf[:, :, :], src_r[:, :, :]))
            link(v.tensor_reduce(out=gmin[:, :], in_=dst_rf[:, :, :], op=ALU.min, axis=AX.X))
            link(v.tensor_reduce(out=gspan[:, :], in_=dst_rf[:, :, :], op=ALU.max, axis=AX.X))
            link(v.tensor_tensor(out=gspan[:, :], in0=gspan[:, :], in1=gmin[:, :], op=ALU.subtract))
            for h in range(2):
                v.tensor_scalar(diag[:, h, :], ident[0:HG, 0:HG], gmin[:, h:h + 1], None, ALU.mult
                                ).then_inc(s_diag, 1)
                v.tensor_scalar(diag[:, 2 + h, :], ident[0:HG, 0:HG], gspan[:, h:h + 1], None, ALU.mult
                                ).then_inc(s_diag, 1)
            dve.wait_ge(s_et, 1)
            for h in range(2):
                for a, to in enumerate((dst_f, src_f)):
                    v.tensor_copy(to[:, h * HG:(h + 1) * HG, :].rearrange("p g j -> p j g"),
                                  ps[:, 2 * h + a, 0:J * HG].rearrange("p (j g) -> p j g", j=J))
            v.tensor_copy(base_f[:, :], ps[:, 4, 0:NG])
            link(v.tensor_reduce(out=span[:, :], in_=ps[0:1, 5, 0:NG], op=ALU.max, axis=AX.X))
            v.tensor_copy(src_i[:, :, :], src_f[:, :, :])
            link(v.tensor_scalar(thr[:, :], thr[:, :], span[:, 0:1], None, ALU.is_le))
            link(v.tensor_reduce(out=rounds_f[:, :], in_=thr[:, :], op=ALU.add, axis=AX.X))
            v.tensor_scalar(rounds_i[:, :], rounds_f[:, :], 1.0, None, ALU.add).then_inc(s_rounds, 1)

            def norm_stats(S):
                with dve.Fori(0, NT) as t:
                    last = v.bn_stats(stats[:, bass.ds(t, 1), :].rearrange("p a k -> p (a k)"),
                                      x_sb[:, bass.ds(t, 1), :].rearrange("p a f -> p (a f)")).then_inc(S["bnst"], 1)
                dve.wait_ge(S["bnst"], NT)

                def st(k):
                    return stats[:, :, k:k + 1].rearrange("p t a -> p (t a)")

                def w(k):
                    return lnw[:, k, :]
                v.tensor_tensor(out=w(0), in0=st(1), in1=st(4), op=ALU.add)
                v.tensor_tensor(out=w(1), in0=st(1), in1=st(4), op=ALU.subtract)
                link(v.tensor_tensor(out=w(2), in0=st(2), in1=st(5), op=ALU.add))
                v.tensor_scalar(w(0), w(0), 0.5, None, ALU.mult)
                v.tensor_scalar(w(2), w(2), 1.0 / D, EPS, ALU.mult, ALU.add)
                link(v.scalar_tensor_tensor(out=w(1), in0=w(1), scalar=0.25, in1=w(1), op0=ALU.mult, op1=ALU.mult))
                v.tensor_tensor(out=w(3), in0=w(2), in1=w(1), op=ALU.add).then_inc(S["var"], 1)
                dve.wait_ge(S["sqrt"], 1)
                link(v.reciprocal(w(7), w(4)))
                link(v.tensor_tensor(out=w(7), in0=w(7), in1=w(3), op=ALU.mult))
                link(v.tensor_tensor(out=w(7), in0=w(7), in1=w(4), op=ALU.add))
                link(v.tensor_scalar(w(7), w(7), 0.5, None, ALU.mult))
                link(v.reciprocal(w(5), w(7)))
                v.scalar_tensor_tensor(out=w(6), in0=w(0), scalar=-1.0, in1=w(5), op0=ALU.mult, op1=ALU.mult
                                       ).then_inc(S["ln"], 1)

            dve.wait_ge(s_x, 32)
            norm_stats(NS[0])

            def keep_T(c, s):
                dve.wait_ge(NS[0]["hT_ps"], c + 1)
                v.tensor_copy(hT[:, bass.ds(c * CW, CW)], ps_f[:, 1024 * s:1024 * s + CW]).then_inc(NS[0]["hT_ok"], 1)

            with dve.Fori(0, NC // 2) as u:
                for s in range(2):
                    keep_T(2 * u + s, s)

            rounds = dve.value_load(rounds_i[0:1, 0:1], min_val=1, max_val=MAXR)

            def first_window(ready):
                v.tensor_copy(base_w[:, :], base_f[0:1, :])
                link(v.tensor_tensor(out=rel_f[:, :, :], in0=dst_f[:, :, :],
                                     in1=base_f[:, :].unsqueeze(2).to_broadcast([P, NG, J]), op=ALU.subtract))
                v.tensor_scalar(base_i[:, :], base_w[:, :], float(ROWS - WIN), None, ALU.min).then_inc(ready, 1)

            def next_window(ready, shifted):
                v.tensor_scalar(base_w[:, :], base_w[:, :], float(WIN), None, ALU.add).then_inc(shifted[0], 1)
                v.tensor_scalar(rel_f[:, :, :], rel_f[:, :, :], float(-WIN), None, ALU.add).then_inc(shifted[0], 1)
                dve.wait_ge(shifted[0], shifted[1])
                v.tensor_scalar(base_i[:, :], base_w[:, :], float(ROWS - WIN), None, ALU.min).then_inc(ready, 1)

            for L in range(2):
                A = AS[L]
                halves = 2 if L == 0 else 1
                v.memset(agg[:, 0:halves, :], 0.0).then_inc(A["added"], 1)
                first_window(A["window"])

                def prepare(r, g, s):
                    v.tensor_copy(idx1[:, s, :], src_i[:, bass.ds(g, 1), :].rearrange("p a j -> p (a j)")
                                  ).then_inc(A["idx"], 1)
                    v.tensor_tensor(out=onehot[:, s, :, :],
                                    in0=iota_w[:, :].unsqueeze(1).to_broadcast([P, J, WIN]),
                                    in1=rel_f[:, bass.ds(g, 1), :].rearrange("p a j -> p j a").to_broadcast(
                                        [P, J, WIN]), op=ALU.is_equal).then_inc(A["onehot"], 1)

                def add(r, g, s):
                    base = dve.value_load(base_i[0:1, bass.ds(g, 1)], min_val=0, max_val=ROWS - WIN)
                    dve.wait_ge(A["psum"], r * NG + g + 1)
                    dve.wait_ge(A["added"], r * NG + g + 1)
                    v.tensor_tensor(out=agg[:, 0:halves, bass.ds(base, WIN)],
                                    in0=agg[:, 0:halves, bass.ds(base, WIN)],
                                    in1=ps[:, s, 0:halves * WIN].rearrange("p (h w) -> p h w", h=halves),
                                    op=ALU.add).then_inc(A["added"], 1)

                with dve.Fori(0, rounds) as r:
                    dve.wait_ge(A["window"], r + 1)
                    for s in range(S1):
                        prepare(r, s, s)
                    with dve.Fori(0, NG // S1 - 1) as u:
                        for s in range(S1):
                            add(r, S1 * u + s, s)
                            prepare(r, S1 * u + S1 + s, s)
                    for s in range(S1):
                        add(r, NG - S1 + s, s)
                    dve.wait_ge(A["added"], r * NG + NG + 1)
                    dve.wait_ge(A["onehot"], r * NG + NG)
                    next_window(A["window"], (A["shift"], 2 * r + 2))
                dve.wait_ge(A["added"], rounds * NG + 1)
                if L == 0:
                    link(v.tensor_scalar(agg[:, 1, :], agg[:, 1, :], 1.0, None, ALU.max))
                    v.reciprocal(agg[:, 1, :], agg[:, 1, :]).then_inc(s_rcnt, 1)
                    dve.wait_ge(s_rcnt, 1)
                nc.vector.sem_inc(A["done"], 1)

                def mean(c, s):
                    v.tensor_tensor(out=mslot[:, s, :], in0=agg[:, 0, bass.ds(c * CW, CW)],
                                    in1=agg[:, 1, bass.ds(c * CW, CW)], op=ALU.mult).then_inc(LS[L]["mean"], 1)

                def finish(c, s):
                    if L == 0:
                        dve.wait_ge(LS[L]["relu"], c + 1)
                        v.tensor_copy(hT[:, bass.ds(c * CW, CW)], tslot[:, s, :]).then_inc(LS[L]["kept"], 1)
                    dve.wait_ge(LS[L]["tr"], c + 1)
                    rows = ps_f[:, 2048 * s + 1024:2048 * s + 1024 + CW].rearrange("p (t f) -> p t f", f=D)
                    if L == 0:
                        v.tensor_copy(hrow[:, s, :, :], rows).then_inc(LS[L]["rows"], 1)
                    else:
                        xs = x_sb[:, bass.ds(c * CT, CT), :]
                        v.tensor_tensor(out=xs, in0=xs, in1=rows, op=ALU.add).then_inc(LS[L]["rows"], 1)

                mean(0, 0)
                mean(1, 1)
                if L == 0:
                    for s in range(2):
                        dve.wait_ge(NS[0]["st"][s], 16 * NC // 2)
                finish(0, 0)
                mean(2, 0)
                finish(1, 1)
                mean(3, 1)
                with dve.Fori(1, NC // 2 - 1) as u:
                    for s in range(2):
                        if L == 0:
                            dve.wait_ge(LS[L]["st"][s], 16 * u)
                        finish(2 * u + s, s)
                        mean(2 * u + 2 + s, s)
                for s in range(2):
                    if L == 0:
                        dve.wait_ge(LS[L]["st"][s], 16 * (NC // 2 - 1))
                    finish(NC - 2 + s, s)

            dve.wait_ge(LS[1]["rows"], NC)
            norm_stats(NS[1])
            first_window(e_window)

            def keep_h3(c, s):
                dve.wait_ge(NS[1]["hrows"], c + 1)
                v.tensor_copy(h3[:, bass.ds(c * CT, CT), :], hrow[:, s, :, :]).then_inc(NS[1]["hT_ok"], 1)
                dve.wait_ge(NS[1]["hT_ps"], c + 1)
                v.tensor_copy(tslot[:, s, :], ps_f[:, 1024 * s:1024 * s + CW]).then_inc(NS[1]["t_ok"], 1)
                dve.wait_ge(NS[1]["t_ok"], c + 1)
                nc.vector.sem_inc(NS[1]["hT_ok"], 1)

            with dve.Fori(0, NC // 2) as u:
                for s in range(2):
                    keep_h3(2 * u + s, s)

            def prepare3(g, s):
                v.tensor_copy(idx1[:, s, :], src_i[:, bass.ds(g, 1), :].rearrange("p a j -> p (a j)")
                              ).then_inc(e_idx, 1)
                v.tensor_copy(src_s[:, s, :], src_f[:, bass.ds(g, 1), :].rearrange("p a j -> p (a j)"))
                v.tensor_tensor(out=onehot[:, s, :, :],
                                in0=iota_w[:, :].unsqueeze(1).to_broadcast([P, J, WIN]),
                                in1=rel_f[:, bass.ds(g, 1), :].rearrange("p a j -> p j a").to_broadcast([P, J, WIN]),
                                op=ALU.is_equal).then_inc(e_onehot, 1)

            SMALL = 8

            def messages(r, g, s):
                it = r * NG + g
                small = [0]

                def chain(instruction):
                    small[0] += 1
                    instruction.then_inc(e_small, 1)
                    dve.wait_ge(e_small, it * SMALL + small[0])

                dve.wait_ge(e_spread, it + 1)
                rel = rel_f[:, bass.ds(g, 1), :].rearrange("p a j -> p (a j)")
                chain(v.tensor_scalar(dupe[:, 0, :], rel, 0.0, None, ALU.is_ge))
                chain(v.scalar_tensor_tensor(out=mask[:, s, :], in0=rel, scalar=float(WIN), in1=dupe[:, 0, :],
                                             op0=ALU.is_lt, op1=ALU.mult))
                v.tensor_tensor(out=eq[:, s, :, :], in0=ps[:, 4 * s, :].rearrange("p (j e) -> p j e", j=J),
                                in1=src_s[:, s, :].unsqueeze(2).to_broadcast([P, J, P]), op=ALU.is_equal
                                ).then_inc(e_eq, 1)
                dve.wait_ge(e_eq, it + 1)
                chain(v.tensor_tensor(out=eqt[:, :, :], in0=eq[:, s, :, :],
                                      in1=tri[:, :].unsqueeze(1).to_broadcast([P, J, P]), op=ALU.mult))
                chain(v.tensor_reduce(out=dupe[:, 1, :], in_=eqt[:, :, :], op=ALU.add, axis=AX.X))
                chain(v.tensor_scalar(dupe[:, 1, :], dupe[:, 1, :], 1.0, None, ALU.min))
                chain(v.tensor_scalar(dupe[:, 2, :], src_s[:, s, :], trash_p[:, 0:1], None, ALU.subtract))
                chain(v.tensor_tensor(out=dupe[:, 2, :], in0=dupe[:, 2, :], in1=dupe[:, 1, :], op=ALU.mult))
                dve.wait_ge(e_turn, it + 1)
                v.tensor_tensor(out=sidx[:, s, :], in0=src_s[:, s, :], in1=dupe[:, 2, :], op=ALU.subtract
                                ).then_inc(e_sidx, 1)
                dve.wait_ge(e_bm, it + 3)
                dve.wait_ge(e_gathered[s], g_count(r, g, s))
                chain(v.tensor_tensor(out=msum[:, s, :, :], in0=rows_g[:, s, :, :],
                                      in1=ps[:, 4 * s + 2, :].rearrange("p (j f) -> p j f", j=J), op=ALU.add))
                nc.vector.sem_inc(e_msum, 1)
                assert small[0] == SMALL

            def g_count(r, g, s):
                return (r * NG + g - s) * (8 * J) + 16 * J

            with dve.Fori(0, rounds) as r:
                dve.wait_ge(e_window, r + 1)
                for s in range(2):
                    prepare3(s, s)
                with dve.Fori(0, NG // 2 - 1) as u:
                    for s in range(2):
                        messages(r, 2 * u + s, s)
                        prepare3(2 * u + 2 + s, s)
                for s in range(2):
                    messages(r, NG - 2 + s, s)
                next_window(e_window, (e_shift, 2 * r + 2))

            def combine(c, s):
                dve.wait_ge(o_acc[s], (c - s) * 16 + 32)
                v.tensor_tensor(out=hrow[:, s, :, :], in0=hrow[:, s, :, :],
                                in1=mslot[:, s, :].rearrange("p (t f) -> p t f", f=D), op=ALU.add).then_inc(o_y1, 1)
                dve.wait_ge(o_y1, c + 1)
                v.scalar_tensor_tensor(out=y_sb[:, s * CT:(s + 1) * CT, :], in0=hrow[:, s, :, :], scalar=0.25,
                                       in1=h3[:, bass.ds(c * CT, CT), :], op0=ALU.mult, op1=ALU.add).then_inc(o_y, 1)

            def residual(c, s):
                dve.wait_ge(o_relu, c + 1)
                v.tensor_tensor(out=abslot[:, s, :, D:2 * D], in0=abslot[:, s, :, D:2 * D],
                                in1=h3[:, bass.ds(c * CT, CT), :], op=ALU.add).then_inc(o_x, 1)
                dve.wait_ge(o_x, c + 1)
                v.tensor_tensor(out=abslot[:, s, :, 0:D], in0=abslot[:, s, :, D:2 * D],
                                in1=x_sb[:, bass.ds(c * CT, CT), :], op=ALU.add).then_inc(o_sum, 1)

            combine(0, 0)
            combine(1, 1)
            for s in range(2):
                residual(s, s)
                combine(2 + s, s)
            with dve.Fori(1, NC // 2 - 1) as u:
                for s in range(2):
                    dve.wait_ge(o_st[s], 16 * u)
                    residual(2 * u + s, s)
                    combine(2 * u + 2 + s, s)
            for s in range(2):
                dve.wait_ge(o_st[s], 16 * (NC // 2 - 1))
                residual(NC - 2 + s, s)


_INS = ['x', 'src', 'dst', 'L0_gnn_W_l0', 'L0_gnn_W_r0', 'L0_gnn_b0', 'L0_gnn_W_l1', 'L0_gnn_W_r1', 'L0_gnn_b1',
        'L1_gnn_W_interact', 'L1_gnn_b_interact', 'L1_gnn_W_update', 'L1_gnn_b_update']


def kernel(**inputs):
    import numpy as _np
    import concourse.bacc as _bacc
    from concourse import mybir as _mybir
    from concourse.bass_utils import run_bass_kernel_spmd as _run

    nc = _bacc.Bacc("TRN2", target_bir_lowering=False, num_devices=1)
    arrays, args = {}, []
    for name in _INS:
        a = _np.ascontiguousarray(inputs[name])
        arrays[f"in_{name}"] = a
        args.append(nc.dram_tensor(f"in_{name}", a.shape, _mybir.dt.from_np(a.dtype), kind="ExternalInput").ap())
    out = nc.dram_tensor("out_0", inputs['x'].shape, _mybir.dt.float32, kind="ExternalOutput").ap()
    gnn_kernel(nc, *args, out)
    r = _run(nc, [arrays], core_ids=[0])
    return r.results[0]["out_0"]
```

```python
import concourse.bass as bass
from concourse import mybir
from contextlib import ExitStack



def gnn_kernel(nc, x, src, dst, W_l0, W_r0, b0, W_l1, W_r1, b1, W_int, b_int, W_upd, b_upd, out):
    f32 = mybir.dt.float32
    i32 = mybir.dt.int32
    ALU = mybir.AluOpType
    ACT = mybir.ActivationFunctionType
    AX = mybir.AxisListType
    P = 128
    N, D = x.shape
    E = src.shape[0]
    EPS = 1e-05
    J = 4
    GE = J * P
    NG = -(-E // GE)
    HG = NG // 2
    WIN = 64
    BUCK = 64
    WIN3 = 2 * BUCK
    S1 = 4
    NB = 2 * (NG // S1 - 1)
    NTILE = NG * J
    LOW = 2048
    TRASH = -(-N // P) * P
    ROWS = TRASH + P
    NT = ROWS // P
    CT = 5
    CW = CT * P
    NC = NT // CT
    HALF = CW // 2
    MAXR = -(-(N + 1) // WIN)
    assert NG == 2 * HG and NG % S1 == 0 and HG <= P and NT == CT * NC and NC % 2 == 0
    assert TRASH + WIN <= ROWS and NC >= 4
    assert NB * BUCK > N and TRASH + WIN3 <= ROWS and N < 4 * LOW and NTILE <= 1024
    HT = NTILE // 2
    PAD = N

    ctx = ExitStack()
    with ctx:
        def sb(name, shape, dt=f32):
            return ctx.enter_context(nc.sbuf_tensor(name, shape, dt))

        def sem(name):
            return ctx.enter_context(nc.semaphore(name))

        def dram(name, shape):
            return nc.dram_tensor(name, shape, f32).ap()

        h0_rows = dram("h0_rows", [ROWS, D])
        h1_rows = dram("h1_rows", [ROWS, D])
        a_rows = dram("a_rows", [ROWS, D])
        b_rows = dram("b_rows", [ROWS, D])

        x_sb = sb("x_sb", [P, NT, D])
        hT = sb("hT", [P, ROWS])
        agg = sb("agg", [P, 2, ROWS])
        gmin = sb("gmin", [HG, 2])
        gspan = sb("gspan", [HG, 2])
        diag = sb("diag", [HG, 4, HG])
        src_i = sb("src_i", [P, NG, J], i32)
        dst_f = sb("dst_f", [P, NG, J])
        rel_f = sb("rel_f", [P, NG, J])
        base_f = sb("base_f", [P, NG])
        base_w = sb("base_w", [1, NG])
        base_i = sb("base_i", [1, NG], i32)
        span = sb("span", [1, 1])
        thr = sb("thr", [1, MAXR])
        reached = sb("reached", [1, MAXR])
        width = sb("width", [1, NG])
        rounds_e = sb("rounds_e", [1, 1], i32)
        rounds_f = sb("rounds_f", [1, 1])
        rounds_i = sb("rounds_i", [1, 1], i32)
        ident = sb("ident", [P, P])
        ones = sb("ones", [P, P])
        upper = sb("upper", [P, P])
        iota_w = sb("iota_w", [P, WIN3])
        f16 = mybir.dt.float16
        src_b = sb("src_b", [P, NTILE])
        place = sb("place", [P, NTILE])
        carry0 = sb("carry0", [P, NTILE])
        carry1 = sb("carry1", [P, NTILE])
        bucket = sb("bucket", [P, NTILE])
        bfirst = sb("bfirst", [P, NG + 1])
        starts = sb("starts", [P, NB + 1])
        bnum = sb("bnum", [P, NB])
        gnum = sb("gnum", [P, NG])
        offset = sb("offset", [P, 1])
        iota_h = sb("iota_h", [P, NTILE], f16)
        iota_l = sb("iota_l", [P, P], f16)
        nought = sb("nought", [P, HT], f16)
        hot_h = sb("hot_h", [P, J, NTILE], f16)
        hot_l = sb("hot_l", [P, J, 2, P], f16)
        wl = [sb("wl0", [P, D]), sb("wl1", [P, D])]
        wr = [sb("wr0", [P, D]), sb("wr1", [P, D])]
        bc = [sb("bc0", [P, 1]), sb("bc1", [P, 1])]
        w_ab = sb("w_ab", [P, 2 * D])
        w_u = sb("w_u", [P, D])
        brow = sb("brow", [1, 3, D])
        stats = sb("stats", [P, NT, 6])
        lnw = sb("lnw", [P, 10, NT])
        idx1 = sb("idx1", [P, S1, J], i32)
        onehot = sb("onehot", [P, S1, J, WIN3])
        rows_g = sb("rows_g", [P, S1, J, D])
        hrow = sb("hrow", [P, 2, CT, D])
        mslot = sb("mslot", [P, 2, CW])
        tslot = sb("tslot", [P, 2, CW])
        abslot = sb("abslot", [P, 2, CT, 2 * D])
        ohT = sb("ohT", [WIN3, 2, GE])
        awin = sb("awin", [WIN3, 2, D])
        msg = sb("msg", [P, 2, J, D])

        src_r = rows_g[0:HG, 0:2, :, :].rearrange("p s j f -> p s (j f)").bitcast(i32)
        dst_r = rows_g[0:HG, 2:4, :, :].rearrange("p s j f -> p s (j f)").bitcast(i32)
        src_rf = mslot[0:HG, :, 0:GE]
        dst_rf = tslot[0:HG, :, 0:GE]
        scratch = abslot[:, :, :, :].rearrange("p s t n -> p (s t n)")
        here = scratch[:, 0:NTILE]
        count = scratch[:, NTILE:2 * NTILE]
        pnum = scratch[:, 2 * NTILE:3 * NTILE]
        ints = count.bitcast(i32)
        src_l = src_i[:, :, :].rearrange("p g j -> p (g j)")
        dst_l = dst_f[:, :, :].rearrange("p g j -> p (g j)")
        assert 3 * NTILE <= 2 * CT * 2 * D and GE <= CW

        ps = ctx.enter_context(nc.psum_tensor("ps", [P, 8, 512], f32))
        ps_f = ps[:, :, :].rearrange("p b n -> p (b n)")

        s_pads = sem("s_pads")
        s_const = sem("s_const")
        s_order = sem("s_order")
        s_edges = sem("s_edges")
        s_x = sem("s_x")
        s_w = sem("s_w")
        s_diag = sem("s_diag")
        s_et = sem("s_et")
        s_dve = sem("s_dve")
        s_rounds = sem("s_rounds")

        def norm_sems(k):
            return {n: sem(f"norm_{n}_{k}") for n in (
                "bnst", "var", "sqrt", "ln", "hrows", "hT_ps", "hT_ok", "kept", "t_ok", "ab_ps", "ab_ok")} | {
                "st": [sem(f"s_st_{k}_{s}") for s in range(2)]}

        def agg_sems(k):
            return {n: sem(f"agg_{n}_{k}") for n in (
                "window", "idx", "onehot", "issue", "psum", "added", "done", "shift")} | {
                "gathered": [sem(f"s_gathered_{k}_{s}") for s in range(S1)]}

        def lin_sems(k):
            return {n: sem(f"lin_{n}_{k}") for n in (
                "mean", "lin", "relu", "kept", "tr", "rows")} | {
                "st": [sem(f"s_lst_{k}_{s}") for s in range(2)]}

        NS = [norm_sems(0), norm_sems(1)]
        AS = [agg_sems(0), agg_sems(1), agg_sems(2)]
        LS = [lin_sems(0), lin_sems(1)]
        s_rcnt = sem("s_rcnt")
        q_scan = sem("q_scan")
        q_off = sem("q_off")
        q_step = sem("q_step")
        q_setup = sem("q_setup")
        q_hot = sem("q_hot")
        q_moved = sem("q_moved")
        q_bucket = sem("q_bucket")
        q_reset = sem("q_reset")
        q_past = sem("q_past")
        q_placed = sem("q_placed")
        q_sorted = sem("q_sorted")
        e_rounds = sem("e_rounds")
        e_loads = sem("e_loads")
        e_awin = [sem(f"e_awin{s}") for s in range(2)]
        e_turned = sem("e_turned")
        e_ohT = sem("e_ohT")
        e_sum = sem("e_sum")
        e_msg = sem("e_msg")
        o_y = sem("o_y")
        o_lin = sem("o_lin")
        o_relu = sem("o_relu")
        o_sum = sem("o_sum")
        o_st = [sem(f"o_st{s}") for s in range(2)]

        block = ctx.enter_context(nc.Block())

        def chunk_rows(table, c):
            return table[bass.ds(c * CW, CW), :].rearrange("(t p) f -> p t f", p=P)

        FULL = (N // P) * P
        LAST = N - FULL
        G1 = (E - HG * GE) // GE
        TAIL = E - (HG + G1) * GE

        @block.sync
        def _(sp):
            sp.wait_ge(s_pads, 4)
            for to, of in ((dst_r, dst), (src_r, src)):
                sp.dma_start(to[:, 0, :], of[0:HG * GE].rearrange("(q e) -> q e", e=GE)).then_inc(s_edges, 16)
                sp.dma_start(to[0:G1, 1, :], of[HG * GE:(HG + G1) * GE].rearrange("(q e) -> q e", e=GE)
                             ).then_inc(s_edges, 16)
                sp.dma_start(to[G1:G1 + 1, 1, 0:TAIL], of[(HG + G1) * GE:E].rearrange("(a e) -> a e", a=1)
                             ).then_inc(s_edges, 16)
            for w, of in ((wl[0], W_l0), (wr[0], W_r0), (wl[1], W_l1), (wr[1], W_r1), (w_u, W_upd)):
                sp.dma_start(w[:, :], of).then_inc(s_w, 16)
            for h in range(2):
                sp.dma_start(w_ab[:, h * D:(h + 1) * D], W_int[h * D:(h + 1) * D, :]).then_inc(s_w, 16)
            sp.dma_start(brow[:, 1, :], b_int.rearrange("(a n) -> a n", a=1)).then_inc(s_w, 16)
            sp.dma_start(brow[:, 2, :], b_upd.rearrange("(a n) -> a n", a=1)).then_inc(s_w, 16)
            sp.dma_start(bc[0][:, :], b0.rearrange("(n a) -> n a", a=1)).then_inc(s_w, 16)
            sp.dma_start(bc[1][:, :], b1.rearrange("(n a) -> n a", a=1)).then_inc(s_w, 16)

            def store_h0(c, s):
                sp.wait_ge(NS[0]["hrows"], c + 1)
                sp.dma_start(chunk_rows(h0_rows, c), hrow[:, s, :, :]).then_inc(NS[0]["st"][s], 16)

            with sp.Fori(0, NC // 2) as u:
                for s in range(2):
                    store_h0(2 * u + s, s)

            def store_h1(c, s):
                sp.wait_ge(LS[0]["rows"], c + 1)
                sp.dma_start(chunk_rows(h1_rows, c), hrow[:, s, :, :]).then_inc(LS[0]["st"][s], 16)

            with sp.Fori(0, NC // 2) as u:
                for s in range(2):
                    store_h1(2 * u + s, s)

            def store_ab(c, s):
                sp.wait_ge(NS[1]["ab_ok"], c + 1)
                sp.dma_start(chunk_rows(a_rows, c), abslot[:, s, :, 0:D]).then_inc(NS[1]["st"][s], 16)
                sp.dma_start(chunk_rows(b_rows, c), abslot[:, s, :, D:2 * D]).then_inc(NS[1]["st"][s], 16)

            with sp.Fori(0, NC // 2) as u:
                for s in range(2):
                    store_ab(2 * u + s, s)
            for s in range(2):
                sp.wait_ge(NS[1]["st"][s], 32 * NC // 2)

            sp.wait_ge(e_rounds, 1)
            rounds = sp.value_load(rounds_e[0:1, 0:1], min_val=1, max_val=MAXR)
            with sp.Fori(0, rounds) as r:
                sp.wait_ge(AS[2]["window"], r + 1)
                sp.sem_inc(e_loads, 1)
                with sp.Fori(0, NG // 2) as u:
                    for s in range(2):
                        base = sp.value_load(base_i[0:1, bass.ds(2 * u + s, 1)], min_val=0, max_val=ROWS - WIN3)
                        sp.wait_ge(e_sum, r * NG + 2 * u + s + 1)
                        sp.dma_start(awin[:, s, :], a_rows[bass.ds(base, WIN3), :]).then_inc(e_awin[s], 16)

            def store_out(c, s):
                sp.wait_ge(o_sum, c + 1)
                sp.dma_start(chunk_rows(out, c), hrow[:, s, :, :]).then_inc(o_st[s], 16)

            with sp.Fori(0, NC // 2 - 1) as u:
                for s in range(2):
                    store_out(2 * u + s, s)
            store_out(NC - 2, 0)
            done = (NC - 1) * CW
            sp.wait_ge(o_sum, NC)
            sp.dma_start(out[done:FULL, :].rearrange("(t p) f -> p t f", p=P),
                         hrow[:, 1, 0:(FULL - done) // P, :]).then_inc(o_st[1], 16)
            sp.dma_start(out[FULL:N, :], hrow[0:LAST, 1, (FULL - done) // P, :]).then_inc(o_st[1], 16)
            sp.wait_ge(o_st[0], 16 * (NC // 2))
            sp.wait_ge(o_st[1], 16 * (NC // 2) + 16)

        @block.gpsimd
        def _(pool):
            nc.gpsimd.memset(src_r[:, 1, :], PAD).then_inc(s_pads, 1)
            nc.gpsimd.memset(dst_r[:, 1, :], PAD).then_inc(s_pads, 1)
            nc.gpsimd.memset(x_sb[:, NT - 2:NT, :], 0.0).then_inc(s_pads, 1)
            nc.gpsimd.memset(brow[:, 0, :], 0.0).then_inc(s_pads, 1)
            nc.gpsimd.memset(ident[:, :], 0.0).then_inc(s_const, 1)
            nc.gpsimd.memset(ones[:, :], 1.0).then_inc(s_const, 1)
            nc.gpsimd.memset(upper[:, :], 1.0).then_inc(s_const, 1)
            nc.gpsimd.iota(iota_w[:, :], pattern=[[1, WIN3]], base=0, channel_multiplier=0,
                           allow_small_or_imprecise_dtypes=True).then_inc(s_const, 1)
            nc.gpsimd.iota(thr[:, :], pattern=[[WIN, MAXR]], base=WIN, channel_multiplier=0,
                           allow_small_or_imprecise_dtypes=True).then_inc(s_const, 1)
            pool.wait_ge(s_const, 4)
            nc.gpsimd.affine_select(out=ident[:, :], in_=ident[:, :], compare_op=ALU.not_equal, fill=1.0,
                                    base=0, pattern=[[-1, P]], channel_multiplier=1).then_inc(s_const, 1)
            nc.gpsimd.affine_select(out=upper[:, :], in_=upper[:, :], compare_op=ALU.is_gt, fill=0.0,
                                    base=0, pattern=[[1, P]], channel_multiplier=-1).then_inc(s_const, 1)

            def numbers(to, pattern, by_partition):
                nc.gpsimd.iota(to, pattern=pattern, base=0, channel_multiplier=by_partition,
                               allow_small_or_imprecise_dtypes=True).then_inc(s_order, 1)

            nc.gpsimd.memset(nought[:, :], 0.0).then_inc(s_order, 1)
            numbers(pnum, [[P, NTILE]], 1)
            numbers(gnum[:, :], [[GE, NG]], 0)
            numbers(bnum[:, :], [[1, NB]], 0)
            numbers(iota_h[:, :], [[1, NTILE]], 0)
            numbers(iota_l[:, :], [[1, P]], 0)
            pool.wait_ge(s_rounds, 1)
            rounds = pool.value_load(rounds_i[0:1, 0:1], min_val=1, max_val=MAXR)

            def aggregate(A, table, rounds):
                with pool.Fori(0, rounds) as r:
                    with pool.Fori(0, NG // S1) as u:
                        for s in range(S1):
                            pool.wait_ge(A["idx"], r * NG + S1 * u + s + 1)
                            pool.sem_inc(A["issue"], 1)
                            for j in range(J):
                                nc.gpsimd.indirect_dma_start(
                                    rows_g[:, s, j, :], None, table,
                                    bass.IndirectOffsetOnAxis(ap=idx1[:, s, j:j + 1], axis=0)
                                ).then_inc(A["gathered"][s], 16)

            for s in range(2):
                pool.wait_ge(NS[0]["st"][s], 16 * NC // 2)
            aggregate(AS[0], h0_rows, rounds)
            for s in range(2):
                pool.wait_ge(LS[0]["st"][s], 16 * NC // 2)
            aggregate(AS[1], h1_rows, rounds)

            for s in range(2):
                pool.wait_ge(NS[1]["st"][s], 32 * NC // 2)
            pool.wait_ge(e_rounds, 1)
            rounds = pool.value_load(rounds_e[0:1, 0:1], min_val=1, max_val=MAXR)
            aggregate(AS[2], b_rows, rounds)

        @block.scalar
        def _(act):
            act.wait_ge(s_pads, 4)
            act.dma_start(x_sb[:, 0:N // P, :], x[0:FULL, :].rearrange("(t p) f -> p t f", p=P)).then_inc(s_x, 16)
            act.dma_start(x_sb[0:LAST, N // P, :], x[FULL:N, :]).then_inc(s_x, 16)

            def norm_scale(S):
                act.wait_ge(S["var"], 1)
                nc.scalar.activation(lnw[:, 4, :], lnw[:, 3, :], ACT.Sqrt).then_inc(S["sqrt"], 1)
                act.wait_ge(S["ln"], 1)

            def norm_rows(S, c, s):
                for k in range(CT):
                    t = c * CT + k
                    last = nc.scalar.activation(
                        hrow[:, s, k, :], x_sb[:, bass.ds(t, 1), :].rearrange("p a f -> p (a f)"), ACT.Relu,
                        bias=lnw[:, 6, bass.ds(t, 1)], scale=lnw[:, 5, bass.ds(t, 1)])
                last.then_inc(S["hrows"], 1)

            norm_scale(NS[0])
            for s in range(2):
                norm_rows(NS[0], s, s)
            with act.Fori(1, NC // 2) as u:
                for s in range(2):
                    act.wait_ge(NS[0]["st"][s], 16 * u)
                    act.wait_ge(NS[0]["hT_ps"], 2 * u + s - 1)
                    norm_rows(NS[0], 2 * u + s, s)

            def linear(L, c, s):
                act.wait_ge(LS[L]["lin"], c + 1)
                nc.scalar.activation(tslot[:, s, :].rearrange("p (h n) -> p h n", h=2),
                                     ps[:, 4 * s:4 * s + 2, 0:HALF], ACT.Relu,
                                     bias=bc[L][:, 0:1]).then_inc(LS[L]["relu"], 1)

            act.wait_ge(s_w, 16 * 11)
            for L in range(2):
                for s in range(2):
                    linear(L, s, s)
                with act.Fori(1, NC // 2) as u:
                    for s in range(2):
                        act.wait_ge(LS[L]["tr"], 2 * u + s - 1)
                        if L == 0:
                            act.wait_ge(LS[L]["kept"], 2 * u + s - 1)
                        linear(L, 2 * u + s, s)

            norm_scale(NS[1])

            def store_ab(c, s):
                act.wait_ge(NS[1]["ab_ps"], c + 1)
                nc.scalar.activation(abslot[:, s, :, :].rearrange("p t n -> p (t n)"), ps_f[:, 2048:2048 + CT * 2 * D],
                                     ACT.Copy).then_inc(NS[1]["ab_ok"], 1)

            def keep_h3T(c, s):
                act.wait_ge(NS[1]["t_ok"], c + 1)
                nc.scalar.activation(agg[:, 1, bass.ds(c * CW, CW)], tslot[:, s, :], ACT.Copy
                                     ).then_inc(NS[1]["kept"], 1)

            for s in range(2):
                norm_rows(NS[1], s, s)
                keep_h3T(s, s)
                if s == 0:
                    act.wait_ge(q_sorted, 1)
                store_ab(s, s)
            with act.Fori(1, NC // 2) as u:
                for s in range(2):
                    act.wait_ge(NS[1]["hT_ok"], 2 * u + s - 1)
                    norm_rows(NS[1], 2 * u + s, s)
                    keep_h3T(2 * u + s, s)
                    act.wait_ge(NS[1]["st"][s], 32 * u)
                    store_ab(2 * u + s, s)

            act.wait_ge(e_rounds, 1)
            rounds = act.value_load(rounds_e[0:1, 0:1], min_val=1, max_val=MAXR)

            def turned(it, g):
                act.wait_ge(e_turned, it + 1)
                nc.scalar.activation(ohT[:, g % 2, :], ps[:, g % 2, :], ACT.Copy).then_inc(e_ohT, 1)

            def messages(it, g):
                act.wait_ge(e_sum, it + 3)
                nc.scalar.activation(msg[:, g % 2, :, :].rearrange("p j f -> p (j f)"), ps[:, 2 + g % 2, :], ACT.Relu
                                     ).then_inc(e_msg, 1)

            with act.Fori(0, rounds) as r:
                turned(r * NG, 0)
                turned(r * NG + 1, 1)
                messages(r * NG, 0)
                with act.Fori(0, NG // 2 - 1) as u:
                    for s in range(2):
                        it = r * NG + 2 * u + s
                        turned(it + 2, s)
                        messages(it + 1, s + 1)
                messages(r * NG + NG - 1, 1)

            def out_steps(c, s):
                act.wait_ge(o_lin, c + 1)
                nc.scalar.activation(hrow[:, s, :, :].rearrange("p t f -> p (t f)"),
                                     ps_f[:, 2048 * s:2048 * s + CW], ACT.Relu).then_inc(o_relu, 1)

            for s in range(2):
                out_steps(s, s)
            with act.Fori(1, NC // 2) as u:
                for s in range(2):
                    act.wait_ge(o_st[s], 16 * u)
                    out_steps(2 * u + s, s)

        @block.tensor
        def _(pe):
            pe.wait_ge(s_const, 7)
            pe.wait_ge(s_diag, 4)
            for h in range(2):
                for a, rows in enumerate((dst_rf, src_rf)):
                    for j in range(J):
                        nc.tensor.transpose(ps[:, 2 * h + a, j * HG:(j + 1) * HG], rows[:, h, j * P:(j + 1) * P],
                                            ident[0:HG, 0:HG])
            for k in range(4):
                last = nc.tensor.matmul(ps[:, 4 + k // 2, (k % 2) * HG:(k % 2 + 1) * HG], ones[0:HG, :],
                                        diag[:, k, :], start=True, stop=True)
            last.then_inc(s_et, 1)

            def norm_transpose(S, c, s):
                pe.wait_ge(S["hrows"], c + 1)
                for k in range(CT):
                    last = nc.tensor.transpose(ps_f[:, 1024 * s + k * P:1024 * s + (k + 1) * P], hrow[:, s, k, :],
                                               ident[:, :])
                last.then_inc(S["hT_ps"], 1)

            pe.wait_ge(s_rounds, 1)
            for s in range(2):
                norm_transpose(NS[0], s, s)
            with pe.Fori(1, NC // 2) as u:
                for s in range(2):
                    pe.wait_ge(NS[0]["hT_ok"], 2 * u + s - 1)
                    norm_transpose(NS[0], 2 * u + s, s)

            rounds = pe.value_load(rounds_i[0:1, 0:1], min_val=1, max_val=MAXR)
            pe.wait_ge(NS[0]["hT_ok"], NC)
            pe.wait_ge(s_w, 16 * 11)

            def group_sum(L, r, u, s):
                A = AS[L]
                pe.wait_ge(A["onehot"], r * NG + S1 * u + s + 1)
                pe.wait_ge(A["gathered"][s], 16 * J * (r * (NG // S1) + u + 1))
                for j in range(J):
                    last = nc.tensor.matmul(ps[:, s, 0:WIN], rows_g[:, s, j, :], onehot[:, s, j, 0:WIN],
                                            start=j == 0, stop=j == J - 1)
                if L == 0:
                    for j in range(J):
                        last = nc.tensor.matmul(ps[:, s, WIN:2 * WIN], ones[:, :], onehot[:, s, j, 0:WIN],
                                                start=j == 0, stop=j == J - 1)
                last.then_inc(A["psum"], 1)

            def bucket_offsets(n):
                pe.wait_ge(q_scan, n + 1)
                nc.tensor.matmul(ps[:, 4, 0:1], upper[:, :], count[:, NTILE - 1:NTILE], start=True, stop=True)
                nc.tensor.matmul(ps[:, 4, 1:2], ones[:, :], count[:, NTILE - 1:NTILE], start=True, stop=True
                                 ).then_inc(q_off, 1)

            def move_edges(tile, j):
                pe.wait_ge(q_hot, tile + 1)
                for c in range(2):
                    for h in range(2):
                        last = nc.tensor.matmul(ps[:, 4 + 2 * c + h, 0:HT], hot_l[:, j, c, :],
                                                hot_h[:, j, h * HT:(h + 1) * HT], start=False, stop=False)
                last.then_inc(q_moved, 1)

            def all_places(first):
                for b in range(4):
                    last = nc.tensor.matmul(ps[:, 4 + b, 0:HT], nought[:, 0:P], nought[:, :],
                                            start=first, stop=not first)
                return last

            for L in range(2):
                A = AS[L]
                if L == 1:
                    pe.wait_ge(LS[0]["rows"], NC)
                    pe.sem_inc(q_moved, J)
                with pe.Fori(0, rounds) as r:
                    if L == 1:
                        all_places(True)
                    with pe.Fori(0, NG // S1 - 1) as u:
                        for s in range(S1):
                            group_sum(L, r, u, s)
                            if L == 0 and s % 2:
                                bucket_offsets(r * NB + 2 * u + s // 2)
                            if L == 1:
                                for j in range(J):
                                    move_edges(r * NTILE + J * (S1 * u + s) + j, j)
                    for s in range(S1):
                        group_sum(L, r, NG // S1 - 1, s)
                        if L == 1:
                            for j in range(J):
                                move_edges(r * NTILE + NTILE - J * (S1 - s) + j, j)
                    if L == 1:
                        all_places(False).then_inc(q_placed, 1)
                pe.wait_ge(A["done"], 1)

                def linear(c, s):
                    pe.wait_ge(LS[L]["mean"], c + 1)
                    for h in range(2):
                        nc.tensor.matmul(ps[:, 4 * s + h, 0:HALF], wl[L][:, :], mslot[:, s, h * HALF:(h + 1) * HALF],
                                         start=True, stop=False)
                        last = nc.tensor.matmul(ps[:, 4 * s + h, 0:HALF], wr[L][:, :],
                                                hT[:, bass.ds(c * CW + h * HALF, HALF)], start=False, stop=True)
                    last.then_inc(LS[L]["lin"], 1)
                    pe.wait_ge(LS[L]["relu"], c + 1)
                    for k in range(CT):
                        last = nc.tensor.transpose(ps_f[:, 2048 * s + 1024 + k * P:2048 * s + 1024 + (k + 1) * P],
                                                   tslot[:, s, k * P:(k + 1) * P], ident[:, :])
                    last.then_inc(LS[L]["tr"], 1)

                for s in range(2):
                    linear(s, s)
                with pe.Fori(1, NC // 2) as u:
                    for s in range(2):
                        pe.wait_ge(LS[L]["rows"], 2 * u + s - 1)
                        linear(2 * u + s, s)

            def ab_step(c, s):
                norm_transpose(NS[1], c, s)
                pe.wait_ge(NS[1]["t_ok"], c + 1)
                for k in range(CT):
                    o = 2048 + k * 2 * D
                    nc.tensor.matmul(ps_f[:, o:o + 2 * D], tslot[:, s, k * P:(k + 1) * P], w_ab[:, :],
                                     start=True, stop=False)
                    last = nc.tensor.matmul(ps_f[:, o:o + 2 * D], ones[0:1, :],
                                            brow[:, 0:2, :].rearrange("p a n -> p (a n)"), start=False, stop=True)
                last.then_inc(NS[1]["ab_ps"], 1)

            ab_step(0, 0)
            pe.wait_ge(NS[1]["ab_ok"], 1)
            ab_step(1, 1)
            with pe.Fori(1, NC // 2) as u:
                for s in range(2):
                    pe.wait_ge(NS[1]["ab_ok"], 2 * u + s)
                    ab_step(2 * u + s, s)
            pe.wait_ge(NS[1]["ab_ok"], NC)

            pe.sem_inc(e_sum, 2)
            pe.wait_ge(e_rounds, 1)
            rounds = pe.value_load(rounds_e[0:1, 0:1], min_val=1, max_val=MAXR)
            A = AS[2]

            def turn(it, s):
                pe.wait_ge(A["onehot"], it + 1)
                for j in range(J):
                    last = nc.tensor.transpose(ps[:, s % 2, j * P:(j + 1) * P], onehot[:, s, j, :], ident[:, :])
                last.then_inc(e_turned, 1)

            def edge_sum(r, it, k, s):
                pe.wait_ge(e_ohT, it + 1)
                pe.wait_ge(e_awin[s % 2], 16 * (r * (NG // 2) + 2 * k + s // 2 + 1))
                pe.wait_ge(A["gathered"][s], 16 * J * (r * (NG // S1) + k + 1))
                for j in range(J):
                    nc.tensor.matmul(ps[:, 2 + s % 2, j * D:(j + 1) * D], ohT[:, s % 2, j * P:(j + 1) * P],
                                     awin[:, s % 2, :], start=True, stop=False)
                    last = nc.tensor.matmul(ps[:, 2 + s % 2, j * D:(j + 1) * D], ident[:, :], rows_g[:, s, j, :],
                                            start=False, stop=True)
                last.then_inc(e_sum, 1)

            def source_sum(it, s):
                pe.wait_ge(e_msg, it + 1)
                for j in range(J):
                    last = nc.tensor.matmul(ps[:, 4 + s % 2, 0:WIN3], msg[:, s % 2, j, :], onehot[:, s, j, :],
                                            start=j == 0, stop=j == J - 1)
                last.then_inc(A["psum"], 1)

            with pe.Fori(0, rounds) as r:
                turn(r * NG, 0)
                turn(r * NG + 1, 1)
                edge_sum(r, r * NG, 0, 0)
                with pe.Fori(0, NG // S1 - 1) as u:
                    for s in range(S1):
                        it = r * NG + S1 * u + s
                        turn(it + 2, (s + 2) % S1)
                        source_sum(it, s)
                        edge_sum(r, it + 1, u + (s + 1) // S1, (s + 1) % S1)
                for s in range(S1):
                    it = r * NG + NG - S1 + s
                    if s + 2 < S1:
                        turn(it + 2, s + 2)
                    else:
                        pe.wait_ge(A["added"], it)
                    source_sum(it, s)
                    if s + 1 < S1:
                        edge_sum(r, it + 1, NG // S1 - 1, s + 1)

            def update(c, s):
                pe.wait_ge(o_y, c + 1)
                for k in range(CT):
                    o = 2048 * s + k * P
                    nc.tensor.matmul(ps_f[:, o:o + P], tslot[:, s, k * P:(k + 1) * P], w_u[:, :],
                                     start=True, stop=False)
                    last = nc.tensor.matmul(ps_f[:, o:o + P], ones[0:1, :], brow[:, 2, :], start=False, stop=True)
                last.then_inc(o_lin, 1)

            for s in range(2):
                update(s, s)
            with pe.Fori(1, NC // 2) as u:
                for s in range(2):
                    pe.wait_ge(o_relu, 2 * u + s - 1)
                    update(2 * u + s, s)

        @block.vector
        def _(dve):
            steps = [0]

            def link(instruction):
                steps[0] += 1
                instruction.then_inc(s_dve, 1)
                dve.wait_ge(s_dve, steps[0])

            v = nc.vector
            dve.wait_ge(s_edges, 16 * 6)
            dve.wait_ge(s_const, 7)
            v.tensor_copy(dst_rf, dst_r)
            link(v.tensor_copy(src_rf, src_r))
            link(v.tensor_reduce(out=gmin[:, :], in_=dst_rf, op=ALU.min, axis=AX.X))
            link(v.tensor_reduce(out=gspan[:, :], in_=dst_rf, op=ALU.max, axis=AX.X))
            link(v.tensor_tensor(out=gspan[:, :], in0=gspan[:, :], in1=gmin[:, :], op=ALU.subtract))
            for h in range(2):
                v.tensor_scalar(diag[:, h, :], ident[0:HG, 0:HG], gmin[:, h:h + 1], None, ALU.mult
                                ).then_inc(s_diag, 1)
                v.tensor_scalar(diag[:, 2 + h, :], ident[0:HG, 0:HG], gspan[:, h:h + 1], None, ALU.mult
                                ).then_inc(s_diag, 1)
            dve.wait_ge(s_et, 1)
            for h in range(2):
                for a, to in enumerate((dst_f, src_i)):
                    v.tensor_copy(to[:, h * HG:(h + 1) * HG, :].rearrange("p g j -> p j g"),
                                  ps[:, 2 * h + a, 0:J * HG].rearrange("p (j g) -> p j g", j=J))
            v.tensor_copy(base_f[:, :], ps[:, 4, 0:NG])
            link(v.tensor_reduce(out=span[:, :], in_=ps[0:1, 5, 0:NG], op=ALU.max, axis=AX.X))
            def count_rounds(to, ready):
                link(v.tensor_scalar(reached[:, :], thr[:, :], span[:, 0:1], None, ALU.is_le))
                link(v.tensor_reduce(out=rounds_f[:, :], in_=reached[:, :], op=ALU.add, axis=AX.X))
                v.tensor_scalar(to[:, :], rounds_f[:, :], 1.0, None, ALU.add).then_inc(ready, 1)

            count_rounds(rounds_i, s_rounds)

            def norm_stats(S):
                with dve.Fori(0, NT) as t:
                    last = v.bn_stats(stats[:, bass.ds(t, 1), :].rearrange("p a k -> p (a k)"),
                                      x_sb[:, bass.ds(t, 1), :].rearrange("p a f -> p (a f)")).then_inc(S["bnst"], 1)
                dve.wait_ge(S["bnst"], NT)

                def st(k):
                    return stats[:, :, k:k + 1].rearrange("p t a -> p (t a)")

                def w(k):
                    return lnw[:, k, :]
                v.tensor_tensor(out=w(0), in0=st(1), in1=st(4), op=ALU.add)
                v.tensor_tensor(out=w(1), in0=st(1), in1=st(4), op=ALU.subtract)
                link(v.tensor_tensor(out=w(2), in0=st(2), in1=st(5), op=ALU.add))
                v.tensor_scalar(w(0), w(0), 0.5, None, ALU.mult)
                v.tensor_scalar(w(2), w(2), 1.0 / D, EPS, ALU.mult, ALU.add)
                link(v.scalar_tensor_tensor(out=w(1), in0=w(1), scalar=0.25, in1=w(1), op0=ALU.mult, op1=ALU.mult))
                v.tensor_tensor(out=w(3), in0=w(2), in1=w(1), op=ALU.add).then_inc(S["var"], 1)
                dve.wait_ge(S["sqrt"], 1)
                link(v.reciprocal(w(7), w(4)))
                link(v.tensor_tensor(out=w(7), in0=w(7), in1=w(3), op=ALU.mult))
                link(v.tensor_tensor(out=w(7), in0=w(7), in1=w(4), op=ALU.add))
                link(v.tensor_scalar(w(7), w(7), 0.5, None, ALU.mult))
                link(v.reciprocal(w(5), w(7)))
                v.scalar_tensor_tensor(out=w(6), in0=w(0), scalar=-1.0, in1=w(5), op0=ALU.mult, op1=ALU.mult
                                       ).then_inc(S["ln"], 1)

            dve.wait_ge(s_x, 32)
            norm_stats(NS[0])

            def keep_T(c, s):
                dve.wait_ge(NS[0]["hT_ps"], c + 1)
                v.tensor_copy(hT[:, bass.ds(c * CW, CW)], ps_f[:, 1024 * s:1024 * s + CW]).then_inc(NS[0]["hT_ok"], 1)

            with dve.Fori(0, NC // 2) as u:
                for s in range(2):
                    keep_T(2 * u + s, s)

            rounds = dve.value_load(rounds_i[0:1, 0:1], min_val=1, max_val=MAXR)

            def window_steps(A, win):
                def first():
                    v.tensor_copy(base_w[:, :], base_f[0:1, :])
                    link(v.tensor_tensor(out=rel_f[:, :, :], in0=dst_f[:, :, :],
                                         in1=base_f[:, :].unsqueeze(2).to_broadcast([P, NG, J]), op=ALU.subtract))
                    v.tensor_scalar(base_i[:, :], base_w[:, :], float(ROWS - win), None, ALU.min
                                    ).then_inc(A["window"], 1)

                def following(r):
                    dve.wait_ge(A["added"], r * NG + NG + 1)
                    dve.wait_ge(A["onehot"], r * NG + NG)
                    v.tensor_scalar(base_w[:, :], base_w[:, :], float(win), None, ALU.add).then_inc(A["shift"], 1)
                    v.tensor_scalar(rel_f[:, :, :], rel_f[:, :, :], float(-win), None, ALU.add
                                    ).then_inc(A["shift"], 1)
                    dve.wait_ge(A["shift"], 2 * r + 2)
                    v.tensor_scalar(base_i[:, :], base_w[:, :], float(ROWS - win), None, ALU.min
                                    ).then_inc(A["window"], 1)
                return first, following

            def group_steps(A, win, halves, bank):
                def prepare(g, s):
                    v.tensor_copy(idx1[:, s, :], src_i[:, bass.ds(g, 1), :].rearrange("p a j -> p (a j)")
                                  ).then_inc(A["idx"], 1)
                    v.tensor_tensor(out=onehot[:, s, :, 0:win],
                                    in0=iota_w[:, 0:win].unsqueeze(1).to_broadcast([P, J, win]),
                                    in1=rel_f[:, bass.ds(g, 1), :].rearrange("p a j -> p j a").to_broadcast(
                                        [P, J, win]), op=ALU.is_equal).then_inc(A["onehot"], 1)

                def add(r, g, s):
                    base = dve.value_load(base_i[0:1, bass.ds(g, 1)], min_val=0, max_val=ROWS - win)
                    dve.wait_ge(A["psum"], r * NG + g + 1)
                    dve.wait_ge(A["added"], r * NG + g + 1)
                    v.tensor_tensor(out=agg[:, 0:halves, bass.ds(base, win)],
                                    in0=agg[:, 0:halves, bass.ds(base, win)],
                                    in1=ps[:, bank(s), 0:halves * win].rearrange("p (h w) -> p h w", h=halves),
                                    op=ALU.add).then_inc(A["added"], 1)
                return prepare, add

            def chained(semaphore, base):
                n = [0]

                def chain(instruction):
                    n[0] += 1
                    instruction.then_inc(semaphore, 1)
                    dve.wait_ge(semaphore, base + n[0])
                return chain, n

            SETUP, STEP, NUMBER = 10, 5, 2

            def places_setup(r):
                chain, n = chained(q_setup, r * SETUP)
                v.memset(place[:, :], 0.0)
                v.memset(starts[:, 0:1], 0.0)
                chain(v.tensor_scalar(ints, src_l, BUCK.bit_length() - 1, None, ALU.arith_shift_right))
                chain(v.tensor_copy(src_b[:, :], ints))
                chain(v.tensor_scalar(ints, src_l, BUCK - 1, None, ALU.bitwise_and))
                chain(v.tensor_scalar(carry1[:, :], ints, 4.0, None, ALU.mult))
                chain(v.tensor_copy(here.bitcast(i32), dst_l))
                chain(v.tensor_scalar(ints, here.bitcast(i32), LOW - 1, None, ALU.bitwise_and))
                chain(v.tensor_copy(carry0[:, :], ints))
                chain(v.tensor_scalar(ints, here.bitcast(i32), LOW.bit_length() - 1, None, ALU.arith_shift_right))
                chain(v.tensor_copy(here, ints))
                chain(v.tensor_tensor(out=carry1[:, :], in0=carry1[:, :], in1=here, op=ALU.add))
                assert n[0] == SETUP
                nc.vector.sem_inc(q_past, 1)

            def count_bucket(r, b):
                chain, n = chained(q_step, (r * NB + b) * STEP)
                start = starts[:, bass.ds(b, 1)]
                chain(v.tensor_scalar(here, src_b[:, :], bnum[:, bass.ds(b, 1)], None, ALU.is_equal))
                v.tensor_tensor_scan(count, ones[:, 0:1].to_broadcast([P, NTILE]), here, 0.0, ALU.mult, ALU.add
                                     ).then_inc(q_scan, 1)
                dve.wait_ge(q_off, r * NB + b + 1)
                chain(v.tensor_scalar(offset[:, :], ps[:, 4, 0:1], start, -1.0, ALU.add, ALU.add))
                chain(v.tensor_scalar(starts[:, bass.ds(b + 1, 1)], ps[:, 4, 1:2], start, None, ALU.add))
                chain(v.scalar_tensor_tensor(out=count, in0=count, scalar=offset[:, 0:1], in1=here,
                                             op0=ALU.add, op1=ALU.mult))
                chain(v.tensor_tensor(out=place[:, :], in0=place[:, :], in1=count, op=ALU.add))
                assert n[0] == STEP
                nc.vector.sem_inc(q_past, 1)

            def number_buckets(r, b):
                start = starts[:, bass.ds(b, 1)]
                v.scalar_tensor_tensor(out=bucket[:, :], in0=pnum, scalar=start, in1=bucket[:, :],
                                       op0=ALU.is_ge, op1=ALU.add).then_inc(q_bucket, 1)
                v.scalar_tensor_tensor(out=bfirst[:, 0:NG], in0=gnum[:, :], scalar=start, in1=bfirst[:, 0:NG],
                                       op0=ALU.is_ge, op1=ALU.add).then_inc(q_bucket, 1)
                dve.wait_ge(q_bucket, (r * NB + b) * NUMBER + NUMBER)
                nc.vector.sem_inc(q_past, 1)

            def hot_places(r, g):
                for j in range(J):
                    tile = J * g + j
                    dve.wait_ge(q_moved, r * NTILE + tile + 1)
                    v.tensor_scalar(hot_h[:, j, :], iota_h[:, :], src_b[:, bass.ds(tile, 1)], None, ALU.is_equal)
                    v.tensor_scalar(hot_l[:, j, 0, :], iota_l[:, :], place[:, bass.ds(tile, 1)],
                                    carry0[:, bass.ds(tile, 1)], ALU.is_equal, ALU.mult)
                    v.tensor_scalar(hot_l[:, j, 1, :], iota_l[:, :], place[:, bass.ds(tile, 1)],
                                    carry1[:, bass.ds(tile, 1)], ALU.is_equal, ALU.mult).then_inc(q_hot, 1)

            for L in range(2):
                A = AS[L]
                halves = 2 if L == 0 else 1
                v.memset(agg[:, 0:halves, :], 0.0).then_inc(A["added"], 1)
                first, following = window_steps(A, WIN)
                prepare, add = group_steps(A, WIN, halves, lambda s: s)
                first()
                with dve.Fori(0, rounds) as r:
                    dve.wait_ge(A["window"], r + 1)
                    for s in range(S1):
                        prepare(s, s)
                    if L == 0:
                        dve.wait_ge(s_order, 6)
                        places_setup(r)
                    else:
                        v.memset(bucket[:, :], -1.0)
                        v.memset(bfirst[:, 0:NG], -1.0).then_inc(q_reset, 1)
                        dve.wait_ge(q_reset, r + 1)
                        nc.vector.sem_inc(q_past, 1)
                    with dve.Fori(0, NG // S1 - 1) as u:
                        for s in range(S1):
                            if L == 1:
                                hot_places(r, S1 * u + s)
                            add(r, S1 * u + s, s)
                            prepare(S1 * u + S1 + s, s)
                            if s % 2:
                                (number_buckets if L else count_bucket)(r, 2 * u + s // 2)
                    for s in range(S1):
                        if L == 1:
                            hot_places(r, NG - S1 + s)
                        add(r, NG - S1 + s, s)
                    following(r)
                dve.wait_ge(A["added"], rounds * NG + 1)
                if L == 0:
                    link(v.tensor_scalar(agg[:, 1, :], agg[:, 1, :], 1.0, None, ALU.max))
                    v.reciprocal(agg[:, 1, :], agg[:, 1, :]).then_inc(s_rcnt, 1)
                    link(v.tensor_copy(ints, place[:, :]))
                    link(v.tensor_scalar(here.bitcast(i32), ints, P.bit_length() - 1, None, ALU.arith_shift_right))
                    v.tensor_copy(src_b[:, :], here.bitcast(i32))
                    link(v.tensor_scalar(ints, ints, P - 1, None, ALU.bitwise_and))
                    link(v.tensor_copy(place[:, :], ints))
                    dve.wait_ge(s_rcnt, 1)
                else:
                    dve.wait_ge(q_placed, rounds)
                    v.tensor_copy(carry0[:, :].rearrange("p (h n) -> p h n", h=2), ps[:, 4:6, 0:HT])
                    link(v.tensor_copy(carry1[:, :].rearrange("p (h n) -> p h n", h=2), ps[:, 6:8, 0:HT]))
                nc.vector.sem_inc(A["done"], 1)

                def mean(c, s):
                    v.tensor_tensor(out=mslot[:, s, :], in0=agg[:, 0, bass.ds(c * CW, CW)],
                                    in1=agg[:, 1, bass.ds(c * CW, CW)], op=ALU.mult).then_inc(LS[L]["mean"], 1)

                def finish(c, s):
                    if L == 0:
                        dve.wait_ge(LS[L]["relu"], c + 1)
                        v.tensor_copy(hT[:, bass.ds(c * CW, CW)], tslot[:, s, :]).then_inc(LS[L]["kept"], 1)
                    dve.wait_ge(LS[L]["tr"], c + 1)
                    rows = ps_f[:, 2048 * s + 1024:2048 * s + 1024 + CW].rearrange("p (t f) -> p t f", f=D)
                    if L == 0:
                        v.tensor_copy(hrow[:, s, :, :], rows).then_inc(LS[L]["rows"], 1)
                    else:
                        xs = x_sb[:, bass.ds(c * CT, CT), :]
                        v.tensor_tensor(out=xs, in0=xs, in1=rows, op=ALU.add).then_inc(LS[L]["rows"], 1)

                mean(0, 0)
                mean(1, 1)
                if L == 0:
                    for s in range(2):
                        dve.wait_ge(NS[0]["st"][s], 16 * NC // 2)
                finish(0, 0)
                mean(2, 0)
                finish(1, 1)
                mean(3, 1)
                with dve.Fori(1, NC // 2 - 1) as u:
                    for s in range(2):
                        if L == 0:
                            dve.wait_ge(LS[L]["st"][s], 16 * u)
                        finish(2 * u + s, s)
                        mean(2 * u + 2 + s, s)
                for s in range(2):
                    if L == 0:
                        dve.wait_ge(LS[L]["st"][s], 16 * (NC // 2 - 1))
                    finish(NC - 2 + s, s)

            dve.wait_ge(LS[1]["rows"], NC)
            norm_stats(NS[1])
            A = AS[2]
            v.memset(agg[:, 0, :], 0.0).then_inc(A["added"], 1)
            link(v.tensor_copy(ints, carry1[:, :]))
            link(v.tensor_scalar(here.bitcast(i32), ints, 3, None, ALU.bitwise_and))
            link(v.tensor_copy(pnum, here.bitcast(i32)))
            link(v.scalar_tensor_tensor(out=src_l, in0=pnum, scalar=float(LOW), in1=carry0[:, :],
                                        op0=ALU.mult, op1=ALU.add))
            link(v.tensor_scalar(here.bitcast(i32), ints, 2, None, ALU.arith_shift_right))
            link(v.tensor_copy(pnum, here.bitcast(i32)))
            v.scalar_tensor_tensor(out=dst_l, in0=bucket[:, :], scalar=float(BUCK), in1=pnum,
                                   op0=ALU.mult, op1=ALU.add).then_inc(q_sorted, 1)
            v.memset(bfirst[:, NG:NG + 1], float(PAD // BUCK))
            link(v.tensor_scalar(base_f[:, :], bfirst[:, 0:NG], float(BUCK), None, ALU.mult))
            link(v.tensor_tensor(out=width[:, :], in0=bfirst[0:1, 1:NG + 1], in1=bfirst[0:1, 0:NG], op=ALU.subtract))
            link(v.tensor_reduce(out=span[:, :], in_=width[:, :], op=ALU.max, axis=AX.X))
            link(v.tensor_scalar(span[:, :], span[:, :], float(BUCK * WIN // WIN3), None, ALU.mult))
            count_rounds(rounds_e, e_rounds)
            dve.wait_ge(e_rounds, 1)
            dve.wait_ge(q_sorted, 1)
            first, following = window_steps(A, WIN3)
            prepare, add = group_steps(A, WIN3, 1, lambda s: 4 + s % 2)
            first()

            def keep_h3(c, s):
                dve.wait_ge(NS[1]["hrows"], c + 1)
                xs = x_sb[:, bass.ds(c * CT, CT), :]
                v.tensor_tensor(out=xs, in0=xs, in1=hrow[:, s, :, :], op=ALU.add).then_inc(NS[1]["hT_ok"], 1)
                dve.wait_ge(NS[1]["hT_ps"], c + 1)
                v.tensor_copy(tslot[:, s, :], ps_f[:, 1024 * s:1024 * s + CW]).then_inc(NS[1]["t_ok"], 1)

            with dve.Fori(0, NC // 2) as u:
                for s in range(2):
                    keep_h3(2 * u + s, s)

            rounds = dve.value_load(rounds_e[0:1, 0:1], min_val=1, max_val=MAXR)
            with dve.Fori(0, rounds) as r:
                dve.wait_ge(A["window"], r + 1)
                for s in range(S1):
                    prepare(s, s)
                with dve.Fori(0, NG // S1 - 1) as u:
                    for s in range(S1):
                        add(r, S1 * u + s, s)
                        prepare(S1 * u + S1 + s, s)
                for s in range(S1):
                    add(r, NG - S1 + s, s)
                following(r)
            dve.wait_ge(A["added"], rounds * NG + 1)
            dve.wait_ge(NS[1]["kept"], NC)

            def update_input(c, s):
                v.scalar_tensor_tensor(out=tslot[:, s, :], in0=agg[:, 0, bass.ds(c * CW, CW)], scalar=0.25,
                                       in1=agg[:, 1, bass.ds(c * CW, CW)], op0=ALU.mult, op1=ALU.add
                                       ).then_inc(o_y, 1)

            def residual(c, s):
                dve.wait_ge(o_relu, c + 1)
                v.tensor_tensor(out=hrow[:, s, :, :], in0=hrow[:, s, :, :], in1=x_sb[:, bass.ds(c * CT, CT), :],
                                op=ALU.add).then_inc(o_sum, 1)

            for s in range(2):
                update_input(s, s)
            with dve.Fori(0, NC // 2 - 1) as u:
                for s in range(2):
                    residual(2 * u + s, s)
                    update_input(2 * u + 2 + s, s)
            for s in range(2):
                residual(NC - 2 + s, s)


_INS = ['x', 'src', 'dst', 'L0_gnn_W_l0', 'L0_gnn_W_r0', 'L0_gnn_b0', 'L0_gnn_W_l1', 'L0_gnn_W_r1', 'L0_gnn_b1',
        'L1_gnn_W_interact', 'L1_gnn_b_interact', 'L1_gnn_W_update', 'L1_gnn_b_update']


def kernel(**inputs):
    import numpy as _np
    import concourse.bacc as _bacc
    from concourse import mybir as _mybir
    from concourse.bass_utils import run_bass_kernel_spmd as _run

    nc = _bacc.Bacc("TRN2", target_bir_lowering=False, num_devices=1)
    arrays, args = {}, []
    for name in _INS:
        a = _np.ascontiguousarray(inputs[name])
        arrays[f"in_{name}"] = a
        args.append(nc.dram_tensor(f"in_{name}", a.shape, _mybir.dt.from_np(a.dtype), kind="ExternalInput").ap())
    out = nc.dram_tensor("out_0", inputs['x'].shape, _mybir.dt.float32, kind="ExternalOutput").ap()
    gnn_kernel(nc, *args, out)
    r = _run(nc, [arrays], core_ids=[0])
    return r.results[0]["out_0"]
```

```python
import concourse.bass as bass
from concourse import mybir
from contextlib import ExitStack



def gnn_kernel(nc, x, src, dst, W_l0, W_r0, b0, W_l1, W_r1, b1, W_int, b_int, W_upd, b_upd, out):
    f32 = mybir.dt.float32
    i32 = mybir.dt.int32
    ALU = mybir.AluOpType
    ACT = mybir.ActivationFunctionType
    AX = mybir.AxisListType
    P = 128
    N, D = x.shape
    E = src.shape[0]
    EPS = 1e-05
    J = 4
    GE = J * P
    NG = -(-E // GE)
    HG = NG // 2
    WIN = 64
    BUCK = 64
    WIN3 = 2 * BUCK
    S1 = 4
    NB = 2 * (NG // S1 - 1)
    NTILE = NG * J
    LOW = 2048
    TRASH = -(-N // P) * P
    ROWS = TRASH + P
    NT = ROWS // P
    CT = 5
    CW = CT * P
    NC = NT // CT
    HALF = CW // 2
    MAXR = -(-(N + 1) // WIN)
    assert NG == 2 * HG and NG % S1 == 0 and HG <= P and NT == CT * NC and NC % 2 == 0
    assert TRASH + WIN <= ROWS and NC >= 4
    assert NB * BUCK > N and TRASH + WIN3 <= ROWS and N < 4 * LOW and NTILE <= 1024
    HT = NTILE // 2
    PAD = N

    ctx = ExitStack()
    with ctx:
        def sb(name, shape, dt=f32):
            return ctx.enter_context(nc.sbuf_tensor(name, shape, dt))

        def sem(name):
            return ctx.enter_context(nc.semaphore(name))

        def dram(name, shape):
            return nc.dram_tensor(name, shape, f32).ap()

        h0_rows = dram("h0_rows", [ROWS, D])
        h1_rows = dram("h1_rows", [ROWS, D])
        a_rows = dram("a_rows", [ROWS, D])
        b_rows = dram("b_rows", [ROWS, D])
        cnt_row = dram("cnt_row", [ROWS])

        x_sb = sb("x_sb", [P, NT, D])
        hT = sb("hT", [P, ROWS])
        agg = sb("agg", [P, 2, ROWS])
        gmin = sb("gmin", [HG, 2])
        gspan = sb("gspan", [HG, 2])
        diag = sb("diag", [HG, 4, HG])
        src_i = sb("src_i", [P, NG, J], i32)
        dst_f = sb("dst_f", [P, NG, J])
        rel_f = sb("rel_f", [P, NG, J])
        base_f = sb("base_f", [P, NG])
        base_w = sb("base_w", [1, NG])
        base_i = sb("base_i", [1, NG], i32)
        span = sb("span", [1, 1])
        thr = sb("thr", [1, MAXR])
        reached = sb("reached", [1, MAXR])
        width = sb("width", [1, NG])
        rounds_e = sb("rounds_e", [1, 1], i32)
        rounds_f = sb("rounds_f", [1, 1])
        rounds_i = sb("rounds_i", [1, 1], i32)
        ident = sb("ident", [P, P])
        ones = sb("ones", [P, P])
        upper = sb("upper", [P, P])
        iota_w = sb("iota_w", [P, WIN3])
        f16 = mybir.dt.float16
        src_b = sb("src_b", [P, NTILE])
        place = sb("place", [P, NTILE])
        carry0 = sb("carry0", [P, NTILE])
        carry1 = sb("carry1", [P, NTILE])
        bucket = sb("bucket", [P, NTILE])
        bfirst = sb("bfirst", [P, NG + 1])
        starts = sb("starts", [P, NB + 1])
        bnum = sb("bnum", [P, NB + 1])
        gnum = sb("gnum", [P, NG])
        offset = sb("offset", [P, 1])
        iota_h = sb("iota_h", [P, NTILE], f16)
        iota_l = sb("iota_l", [P, P], f16)
        nought = sb("nought", [P, HT], f16)
        hot_h = sb("hot_h", [P, J, NTILE], f16)
        hot_l = sb("hot_l", [P, J, 2, P], f16)
        wl = [sb("wl0", [P, D]), sb("wl1", [P, D])]
        wr = [sb("wr0", [P, D]), sb("wr1", [P, D])]
        bc = [sb("bc0", [P, 1]), sb("bc1", [P, 1])]
        w_ab = sb("w_ab", [P, 2 * D])
        w_u = sb("w_u", [P, D])
        bias = sb("bias", [P, 2, D])
        cnt_cols = sb("cnt_cols", [P, NT])
        stats = sb("stats", [P, NT, 6])
        lnw = sb("lnw", [P, 10, NT])
        idx1 = sb("idx1", [P, S1, J], i32)
        onehot = sb("onehot", [P, S1, J, WIN3])
        rows_g = sb("rows_g", [P, S1, J, D])
        hrow = sb("hrow", [P, 2, CT, D])
        mslot = sb("mslot", [P, 2, CW])
        tslot = sb("tslot", [P, 2, CW])
        abslot = sb("abslot", [P, 2, CT, 2 * D])
        ohT = sb("ohT", [WIN3, 2, GE])
        awin = sb("awin", [WIN3, 2, D])
        msg = sb("msg", [P, 2, J, D])

        src_r = rows_g[0:HG, 0:2, :, :].rearrange("p s j f -> p s (j f)").bitcast(i32)
        dst_r = rows_g[0:HG, 2:4, :, :].rearrange("p s j f -> p s (j f)").bitcast(i32)
        src_rf = mslot[0:HG, :, 0:GE]
        dst_rf = tslot[0:HG, :, 0:GE]
        pslot = onehot[:, :, :, :].rearrange("p s j w -> p (s j w)")[:, 0:2 * CW].rearrange("p (s n) -> p s n", s=2)
        assert 2 * CW <= S1 * J * WIN3
        scratch = abslot[:, :, :, :].rearrange("p s t n -> p (s t n)")
        hot_v = hot_h[:, :, :].rearrange("p j n -> p (j n)").bitcast(f32)
        heres = [scratch[:, 0:NTILE], hot_v[:, 0:NTILE]]
        counts = [scratch[:, NTILE:2 * NTILE], hot_v[:, NTILE:2 * NTILE]]
        here, count = heres[0], counts[0]
        pnum = scratch[:, 2 * NTILE:3 * NTILE]
        ints = count.bitcast(i32)
        gone = heres[1]
        src_l = src_i[:, :, :].rearrange("p g j -> p (g j)")
        dst_l = dst_f[:, :, :].rearrange("p g j -> p (g j)")
        assert 3 * NTILE <= 2 * CT * 2 * D and GE <= CW and J == 4

        ps = ctx.enter_context(nc.psum_tensor("ps", [P, 8, 512], f32))
        ps_f = ps[:, :, :].rearrange("p b n -> p (b n)")

        s_pads = sem("s_pads")
        s_const = sem("s_const")
        s_order = sem("s_order")
        s_edges = sem("s_edges")
        s_x = [sem(f"s_x{k}") for k in range(2)]
        s_w = sem("s_w")
        s_diag = sem("s_diag")
        s_et = sem("s_et")
        s_dve = sem("s_dve")
        s_rounds = sem("s_rounds")
        p_past = sem("p_past")

        def norm_sems(k):
            return {n: sem(f"norm_{n}_{k}") for n in (
                "bnst", "var", "sqrt", "ln", "hrows", "hT_ps", "hT_ok", "kept", "t_ok", "product", "rows",
                "a_ps", "b_ps", "a_ok", "b_ok")} | {
                "st": [sem(f"s_st_{k}_{s}") for s in range(2)], "st_b": [sem(f"s_stb_{k}_{s}") for s in range(2)]}

        def agg_sems(k):
            return {n: sem(f"agg_{n}_{k}") for n in (
                "window", "idx", "onehot", "issue", "psum", "added", "done", "shift")} | {
                "gathered": [sem(f"s_gathered_{k}_{s}") for s in range(S1)]}

        def lin_sems(k):
            return {n: sem(f"lin_{n}_{k}") for n in (
                "own", "own_ok", "mean", "odd", "relu", "kept", "tr", "rows")} | {
                "st": [sem(f"s_lst_{k}_{s}") for s in range(2)],
                "sum": [sem(f"lin_sum_{k}_{s}") for s in range(2)]}

        NS = [norm_sems(0), norm_sems(1)]
        AS = [agg_sems(0), agg_sems(1), agg_sems(2)]
        LS = [lin_sems(0), lin_sems(1)]
        s_crow = sem("s_crow")
        s_cnt = sem("s_cnt")
        s_first = sem("s_first")
        s_rcnt = sem("s_rcnt")
        s_rrow = sem("s_rrow")
        s_spread = [sem(f"s_spread{k}") for k in range(3)]
        q_scan = sem("q_scan")
        q_off = sem("q_off")
        q_step = sem("q_step")
        q_setup = sem("q_setup")
        q_hot = sem("q_hot")
        q_moved = sem("q_moved")
        q_past = sem("q_past")
        q_placed = sem("q_placed")
        q_carried = sem("q_carried")
        q_cut = sem("q_cut")
        q_sorted = sem("q_sorted")
        e_rounds = sem("e_rounds")
        e_loads = sem("e_loads")
        e_awin = [sem(f"e_awin{s}") for s in range(2)]
        e_turned = sem("e_turned")
        e_ohT = sem("e_ohT")
        e_sum = sem("e_sum")
        e_msg = sem("e_msg")
        e_done = sem("e_done")
        o_y = sem("o_y")
        o_lin = sem("o_lin")
        o_biased = sem("o_biased")
        o_sum = sem("o_sum")
        o_st = sem("o_st")

        block = ctx.enter_context(nc.Block())

        def chunk_rows(table, c):
            return table[bass.ds(c * CW, CW), :].rearrange("(t p) f -> p t f", p=P)

        SPREAD = ((2, 4), (4, NC), (0, 2))
        X_EARLY = 4 * CT
        FULL = (N // P) * P
        LAST = N - FULL
        G1 = (E - HG * GE) // GE
        TAIL = E - (HG + G1) * GE

        @block.sync
        def _(sp):
            sp.wait_ge(s_pads, 3)
            for to, of in ((dst_r, dst), (src_r, src)):
                sp.dma_start(to[:, 0, :], of[0:HG * GE].rearrange("(q e) -> q e", e=GE)).then_inc(s_edges, 16)
                sp.dma_start(to[0:G1, 1, :], of[HG * GE:(HG + G1) * GE].rearrange("(q e) -> q e", e=GE)
                             ).then_inc(s_edges, 16)
                sp.dma_start(to[G1:G1 + 1, 1, 0:TAIL], of[(HG + G1) * GE:E].rearrange("(a e) -> a e", a=1)
                             ).then_inc(s_edges, 16)
            early = X_EARLY * P
            sp.dma_start(x_sb[:, 0:X_EARLY, :], x[0:early, :].rearrange("(t p) f -> p t f", p=P)
                         ).then_inc(s_x[0], 16)
            sp.dma_start(x_sb[:, X_EARLY:N // P, :], x[early:FULL, :].rearrange("(t p) f -> p t f", p=P)
                         ).then_inc(s_x[1], 16)
            sp.dma_start(x_sb[0:LAST, N // P, :], x[FULL:N, :]).then_inc(s_x[1], 16)

            def store_h0(c, s):
                sp.wait_ge(NS[0]["rows"], c + 1)
                sp.dma_start(chunk_rows(h0_rows, c), mslot[:, s, :].rearrange("p (t f) -> p t f", f=D)
                             ).then_inc(NS[0]["st"][s], 16)

            with sp.Fori(0, NC // 2) as u:
                for s in range(2):
                    store_h0(2 * u + s, s)

            sp.wait_ge(AS[0]["done"], 1)
            sp.dma_start(cnt_row.rearrange("(a n) -> a n", a=1), agg[0:1, 1, :]).then_inc(s_crow, 16)
            sp.wait_ge(s_crow, 16)
            sp.dma_start(cnt_cols[:, :], cnt_row.rearrange("(p t) -> p t", t=NT)).then_inc(s_cnt, 16)
            sp.wait_ge(s_rcnt, 1)
            sp.dma_start(cnt_row.rearrange("(p t) -> p t", t=NT), cnt_cols[:, :]).then_inc(s_rrow, 16)
            sp.wait_ge(s_rrow, 16)
            for k, (c0, c1) in enumerate(SPREAD):
                if c0 == 0:
                    sp.wait_ge(s_first, 2)
                sp.dma_start(agg[:, 1, c0 * CW:c1 * CW],
                             cnt_row[c0 * CW:c1 * CW].rearrange("(a n) -> a n", a=1).to_broadcast([P, (c1 - c0) * CW])
                             ).then_inc(s_spread[k], 16)

            def store_h1(c, s):
                sp.wait_ge(LS[0]["rows"], c + 1)
                sp.dma_start(chunk_rows(h1_rows, c), hrow[:, s, :, :]).then_inc(LS[0]["st"][s], 16)

            with sp.Fori(0, NC // 2) as u:
                for s in range(2):
                    store_h1(2 * u + s, s)

            def store_ab(c, s):
                sp.wait_ge(NS[1]["b_ok"], c + 1)
                sp.dma_start(chunk_rows(b_rows, c), abslot[:, s, :, D:2 * D]).then_inc(NS[1]["st_b"][s], 16)
                sp.wait_ge(NS[1]["a_ok"], c + 1)
                sp.dma_start(chunk_rows(a_rows, c), abslot[:, s, :, 0:D]).then_inc(NS[1]["st"][s], 16)

            with sp.Fori(0, NC // 2) as u:
                for s in range(2):
                    store_ab(2 * u + s, s)
            for s in range(2):
                sp.wait_ge(NS[1]["st"][s], 16 * NC // 2)

            sp.wait_ge(e_rounds, 1)
            rounds = sp.value_load(rounds_e[0:1, 0:1], min_val=1, max_val=MAXR)
            with sp.Fori(0, rounds) as r:
                sp.wait_ge(AS[2]["window"], r + 1)
                sp.sem_inc(e_loads, 1)
                with sp.Fori(0, NG // 2) as u:
                    for s in range(2):
                        base = sp.value_load(base_i[0:1, bass.ds(2 * u + s, 1)], min_val=0, max_val=ROWS - WIN3)
                        sp.wait_ge(e_sum, r * NG + 2 * u + s + 1)
                        sp.dma_start(awin[:, s, :], a_rows[bass.ds(base, WIN3), :]).then_inc(e_awin[s], 16)

            with sp.Fori(0, NC - 1) as c:
                sp.wait_ge(o_sum, c + 1)
                sp.dma_start(chunk_rows(out, c), x_sb[:, bass.ds(c * CT, CT), :]).then_inc(o_st, 16)
            done = (NC - 1) * CW
            sp.wait_ge(o_sum, NC)
            sp.dma_start(out[done:FULL, :].rearrange("(t p) f -> p t f", p=P),
                         x_sb[:, done // P:FULL // P, :]).then_inc(o_st, 16)
            sp.dma_start(out[FULL:N, :], x_sb[0:LAST, FULL // P, :]).then_inc(o_st, 16)
            sp.wait_ge(o_st, 16 * (NC + 1))

        @block.gpsimd
        def _(pool):
            nc.gpsimd.memset(src_r[:, 1, :], PAD).then_inc(s_pads, 1)
            nc.gpsimd.memset(dst_r[:, 1, :], PAD).then_inc(s_pads, 1)
            nc.gpsimd.memset(x_sb[:, NT - 2:NT, :], 0.0).then_inc(s_pads, 1)
            nc.gpsimd.memset(ident[:, :], 0.0).then_inc(s_const, 1)
            nc.gpsimd.memset(ones[:, :], 1.0).then_inc(s_const, 1)
            nc.gpsimd.memset(upper[:, :], 1.0).then_inc(s_const, 1)
            nc.gpsimd.iota(iota_w[:, :], pattern=[[1, WIN3]], base=0, channel_multiplier=0,
                           allow_small_or_imprecise_dtypes=True).then_inc(s_const, 1)
            nc.gpsimd.iota(thr[:, :], pattern=[[WIN, MAXR]], base=WIN, channel_multiplier=0,
                           allow_small_or_imprecise_dtypes=True).then_inc(s_const, 1)
            pool.wait_ge(s_const, 4)
            nc.gpsimd.affine_select(out=ident[:, :], in_=ident[:, :], compare_op=ALU.not_equal, fill=1.0,
                                    base=0, pattern=[[-1, P]], channel_multiplier=1).then_inc(s_const, 1)
            nc.gpsimd.affine_select(out=upper[:, :], in_=upper[:, :], compare_op=ALU.is_gt, fill=0.0,
                                    base=0, pattern=[[1, P]], channel_multiplier=-1).then_inc(s_const, 1)

            def numbers(to, pattern, by_partition):
                nc.gpsimd.iota(to, pattern=pattern, base=0, channel_multiplier=by_partition,
                               allow_small_or_imprecise_dtypes=True).then_inc(s_order, 1)

            nc.gpsimd.memset(nought[:, :], 0.0).then_inc(s_order, 1)
            numbers(pnum, [[P, NTILE]], 1)
            numbers(gnum[:, :], [[GE, NG]], 0)
            numbers(bnum[:, :], [[1, NB + 1]], 0)
            numbers(iota_h[:, :], [[1, NTILE]], 0)
            numbers(iota_l[:, :], [[1, P]], 0)
            nc.gpsimd.memset(agg[:, :, :], 0.0).then_inc(AS[0]["added"], 1)
            pool.wait_ge(s_rounds, 1)
            rounds = pool.value_load(rounds_i[0:1, 0:1], min_val=1, max_val=MAXR)

            def aggregate(A, table, rounds):
                with pool.Fori(0, rounds) as r:
                    with pool.Fori(0, NG // S1) as u:
                        for s in range(S1):
                            pool.wait_ge(A["idx"], r * NG + S1 * u + s + 1)
                            pool.sem_inc(A["issue"], 1)
                            for j in range(J):
                                nc.gpsimd.indirect_dma_start(
                                    rows_g[:, s, j, :], None, table,
                                    bass.IndirectOffsetOnAxis(ap=idx1[:, s, j:j + 1], axis=0)
                                ).then_inc(A["gathered"][s], 16)

            for s in range(2):
                pool.wait_ge(NS[0]["st"][s], 16 * NC // 2)
            aggregate(AS[0], h0_rows, rounds)

            def means(L):
                def mean(c, s, count, done):
                    nc.gpsimd.tensor_tensor(out=pslot[:, s, :], in0=agg[:, 0, bass.ds(c * CW, CW)], in1=count,
                                            op=ALU.mult).then_inc(LS[L][done], 1)

                def odd_total(u):
                    pool.wait_ge(LS[1]["odd"], u + 1)
                    nc.gpsimd.tensor_tensor(out=mslot[:, 1, :], in0=pslot[:, 1, :],
                                            in1=hT[:, bass.ds((2 * u + 1) * CW, CW)], op=ALU.add
                                            ).then_inc(LS[1]["sum"][1], 1)

                def inverse(c):
                    return agg[:, 1, bass.ds(c * CW, CW)]

                pool.wait_ge(AS[L]["done"], 1)
                if L == 0:
                    pool.wait_ge(s_first, 1)
                    mean(0, 0, tslot[:, 0, :], "mean")
                    pool.wait_ge(s_spread[0], 16)
                    pool.wait_ge(LS[0]["sum"][0], 1)
                    mean(2, 0, inverse(2), "mean")
                    pool.wait_ge(s_spread[1], 16)
                    with pool.Fori(2, NC // 2) as u:
                        pool.wait_ge(LS[0]["sum"][0], u)
                        mean(2 * u, 0, inverse(2 * u), "mean")
                else:
                    pool.wait_ge(s_spread[2], 16)
                    pool.wait_ge(LS[1]["own_ok"], NC)
                    mean(0, 0, inverse(0), "mean")
                    mean(1, 1, inverse(1), "odd")
                    odd_total(0)
                    with pool.Fori(1, NC // 2) as u:
                        pool.wait_ge(LS[1]["sum"][0], u)
                        mean(2 * u, 0, inverse(2 * u), "mean")
                        pool.wait_ge(LS[1]["sum"][1], u)
                        mean(2 * u + 1, 1, inverse(2 * u + 1), "odd")
                        pool.wait_ge(LS[1]["relu"], 2 * u)
                        odd_total(u)
                pool.wait_ge(LS[L]["mean"], NC // 2)
                pool.wait_ge(LS[L]["sum"][1], NC // 2)

            means(0)
            nc.gpsimd.memset(agg[:, 0, :], 0.0).then_inc(AS[1]["added"], 1)
            for s in range(2):
                pool.wait_ge(LS[0]["st"][s], 16 * NC // 2)
            aggregate(AS[1], h1_rows, rounds)

            means(1)

            def keep_h3T(c, s):
                pool.wait_ge(NS[1]["t_ok"], c + 1)
                pool.sem_inc(p_past, 1)
                nc.gpsimd.tensor_copy(agg[:, 0, bass.ds(c * CW, CW)], tslot[:, s, :]).then_inc(NS[1]["kept"], 1)

            with pool.Fori(0, NC // 2) as u:
                for s in range(2):
                    keep_h3T(2 * u + s, s)

            for s in range(2):
                pool.wait_ge(NS[1]["st_b"][s], 16 * NC // 2)
            pool.wait_ge(e_rounds, 1)
            rounds = pool.value_load(rounds_e[0:1, 0:1], min_val=1, max_val=MAXR)
            aggregate(AS[2], b_rows, rounds)

        @block.scalar
        def _(act):
            act.wait_ge(s_edges, 16 * 6)
            for w, of in ((wl[0], W_l0), (wr[0], W_r0), (wl[1], W_l1), (wr[1], W_r1), (w_u, W_upd)):
                act.dma_start(w[:, :], of).then_inc(s_w, 16)
            for h in range(2):
                act.dma_start(w_ab[:, h * D:(h + 1) * D], W_int[h * D:(h + 1) * D, :]).then_inc(s_w, 16)
            for k, of in enumerate((b_int, b_upd)):
                act.dma_start(bias[:, k, :], of.rearrange("(a n) -> a n", a=1).to_broadcast([P, D])).then_inc(s_w, 16)
            act.dma_start(bc[0][:, :], b0.rearrange("(n a) -> n a", a=1)).then_inc(s_w, 16)
            act.dma_start(bc[1][:, :], b1.rearrange("(n a) -> n a", a=1)).then_inc(s_w, 16)

            def norm_scale(S):
                act.wait_ge(S["var"], 1)
                nc.scalar.activation(lnw[:, 4, :], lnw[:, 3, :], ACT.Sqrt).then_inc(S["sqrt"], 1)
                act.wait_ge(S["ln"], 1)

            def norm_rows(S, c, s):
                for k in range(CT):
                    t = c * CT + k
                    last = nc.scalar.activation(
                        hrow[:, s, k, :], x_sb[:, bass.ds(t, 1), :].rearrange("p a f -> p (a f)"), ACT.Relu,
                        bias=lnw[:, 6, bass.ds(t, 1)], scale=lnw[:, 5, bass.ds(t, 1)])
                last.then_inc(S["hrows"], 1)

            norm_scale(NS[0])
            for s in range(2):
                norm_rows(NS[0], s, s)
            with act.Fori(1, NC // 2) as u:
                for s in range(2):
                    act.wait_ge(NS[0]["hT_ps"], 2 * u + s - 1)
                    norm_rows(NS[0], 2 * u + s, s)

            act.wait_ge(s_rounds, 1)
            rounds = act.value_load(rounds_i[0:1, 0:1], min_val=1, max_val=MAXR)
            act.wait_ge(s_w, 16 * 11)

            def indices(A, g, s):
                nc.scalar.activation(idx1[:, s, :], src_i[:, bass.ds(g, 1), :].rearrange("p a j -> p (a j)"),
                                     ACT.Copy).then_inc(A["idx"], 1)

            for L in range(2):
                A = AS[L]

                def own_part(c, s):
                    act.wait_ge(LS[L]["own"], c + 1)
                    nc.scalar.activation(hT[:, bass.ds(c * CW, CW)].rearrange("p (h n) -> p h n", h=2),
                                         ps[:, 4 + 2 * s:6 + 2 * s, 0:HALF], ACT.Identity,
                                         bias=bc[L][:, 0:1]).then_inc(LS[L]["own_ok"], 1)

                def rectify(u, s):
                    c = 2 * u + s
                    act.wait_ge(LS[L]["sum"][s], u + 1)
                    nc.scalar.activation(tslot[:, s, :], mslot[:, s, :], ACT.Relu).then_inc(LS[L]["relu"], 1)
                    if L == 0:
                        nc.scalar.activation(hT[:, bass.ds(c * CW, CW)], mslot[:, s, :], ACT.Relu
                                             ).then_inc(LS[L]["kept"], 1)

                for s in range(S1):
                    indices(A, s, s)
                with act.Fori(0, NC // 2) as u:
                    for s in range(2):
                        own_part(2 * u + s, s)
                with act.Fori(0, rounds) as r:
                    with act.Fori(0, NG // S1 - 1) as u:
                        for s in range(S1):
                            act.wait_ge(A["psum"], r * NG + S1 * u + s + 1)
                            indices(A, S1 * u + S1 + s, s)
                    for s in range(S1):
                        act.wait_ge(A["psum"], r * NG + NG - S1 + s + 1)
                        indices(A, s, s)
                if L == 1:
                    act.wait_ge(q_placed, rounds)
                    act.sem_inc(q_carried, 1)
                    nc.scalar.activation(carry1[:, :].bitcast(i32).rearrange("p (h n) -> p h n", h=2),
                                         ps[:, 6:8, 0:HT], ACT.Copy).then_inc(q_carried, 1)
                    nc.scalar.activation(carry0[:, :].rearrange("p (h n) -> p h n", h=2),
                                         ps[:, 4:6, 0:HT], ACT.Copy).then_inc(q_carried, 1)
                for s in range(2):
                    rectify(0, s)
                    if L == 1:
                        act.wait_ge(q_cut, s + 1)
                        nc.scalar.activation((pnum, gone)[s], (here, ints)[s].bitcast(i32), ACT.Copy
                                             ).then_inc(q_carried, 1)
                with act.Fori(1, NC // 2) as u:
                    for s in range(2):
                        act.wait_ge(LS[L]["tr"], 2 * u + s - 1)
                        rectify(u, s)

            norm_scale(NS[1])

            def a_part(c, s):
                act.wait_ge(NS[1]["a_ps"], c + 1)
                nc.scalar.activation(abslot[:, s, :, 0:D], ps_f[:, 2048:2048 + CW].rearrange("p (t f) -> p t f", f=D),
                                     ACT.Copy).then_inc(NS[1]["a_ok"], 1)

            for s in range(2):
                norm_rows(NS[1], s, s)
            act.wait_ge(q_sorted, 1)
            for s in range(2):
                act.wait_ge(NS[1]["t_ok"], s + 1)
                norm_rows(NS[1], 2 + s, s)
                a_part(s, s)
            with act.Fori(1, NC // 2 - 1) as u:
                for s in range(2):
                    act.wait_ge(NS[1]["t_ok"], 2 * u + s + 1)
                    norm_rows(NS[1], 2 * u + 2 + s, s)
                    act.wait_ge(NS[1]["st"][s], 16 * u)
                    a_part(2 * u + s, s)
            for s in range(2):
                act.wait_ge(NS[1]["st"][s], 16 * (NC // 2 - 1))
                a_part(NC - 2 + s, s)

            act.wait_ge(e_rounds, 1)
            rounds = act.value_load(rounds_e[0:1, 0:1], min_val=1, max_val=MAXR)

            def turned(it, g):
                act.wait_ge(e_turned, it + 1)
                nc.scalar.activation(ohT[:, g % 2, :], ps[:, g % 2, :], ACT.Copy).then_inc(e_ohT, 1)

            def messages(it, g):
                act.wait_ge(e_sum, it + 3)
                nc.scalar.activation(msg[:, g % 2, :, :].rearrange("p j f -> p (j f)"), ps[:, 2 + g % 2, :], ACT.Relu,
                                     scale=0.25).then_inc(e_msg, 1)

            with act.Fori(0, rounds) as r:
                turned(r * NG, 0)
                turned(r * NG + 1, 1)
                messages(r * NG, 0)
                with act.Fori(0, NG // 2 - 1) as u:
                    for s in range(2):
                        it = r * NG + 2 * u + s
                        turned(it + 2, s)
                        messages(it + 1, s + 1)
                messages(r * NG + NG - 1, 1)

            def update_input(c, s):
                nc.scalar.activation(tslot[:, s, :], agg[:, 0, bass.ds(c * CW, CW)], ACT.Copy).then_inc(o_y, 1)

            act.wait_ge(e_done, 1)
            for s in range(2):
                update_input(s, s)
            with act.Fori(1, NC // 2) as u:
                for s in range(2):
                    act.wait_ge(o_lin, 2 * u + s - 1)
                    update_input(2 * u + s, s)

        @block.tensor
        def _(pe):
            pe.wait_ge(s_const, 7)
            pe.wait_ge(s_diag, 4)
            for h in range(2):
                for a, rows in enumerate((dst_rf, src_rf)):
                    for j in range(J):
                        nc.tensor.transpose(ps[:, 2 * h + a, j * HG:(j + 1) * HG], rows[:, h, j * P:(j + 1) * P],
                                            ident[0:HG, 0:HG])
            for k in range(4):
                last = nc.tensor.matmul(ps[:, 4 + k // 2, (k % 2) * HG:(k % 2 + 1) * HG], ones[0:HG, :],
                                        diag[:, k, :], start=True, stop=True)
            last.then_inc(s_et, 1)

            def norm_transpose(S, c, s):
                pe.wait_ge(S["hrows"], c + 1)
                for k in range(CT):
                    last = nc.tensor.transpose(ps_f[:, 1024 * s + k * P:1024 * s + (k + 1) * P], hrow[:, s, k, :],
                                               ident[:, :])
                last.then_inc(S["hT_ps"], 1)

            pe.wait_ge(s_rounds, 1)
            pe.wait_ge(s_w, 16 * 11)

            def row_product(S, c, s, w):
                pe.wait_ge(S["t_ok"], c + 1)
                for k in range(CT):
                    o = 2048 + 1024 * s + k * P
                    last = nc.tensor.matmul(ps_f[:, o:o + P], tslot[:, s, k * P:(k + 1) * P], w[:, :],
                                            start=True, stop=True)
                last.then_inc(S["product"], 1)

            for s in range(2):
                norm_transpose(NS[0], s, s)
            for s in range(2):
                row_product(NS[0], s, s, wl[0])
                norm_transpose(NS[0], 2 + s, s)
            with pe.Fori(1, NC // 2 - 1) as u:
                for s in range(2):
                    pe.wait_ge(NS[0]["rows"], 2 * u + s - 1)
                    row_product(NS[0], 2 * u + s, s, wl[0])
                    norm_transpose(NS[0], 2 * u + 2 + s, s)
            for s in range(2):
                pe.wait_ge(NS[0]["rows"], NC - 3 + s)
                row_product(NS[0], NC - 2 + s, s, wl[0])

            rounds = pe.value_load(rounds_i[0:1, 0:1], min_val=1, max_val=MAXR)
            pe.wait_ge(NS[0]["rows"], NC)
            pe.wait_ge(NS[0]["kept"], NC)

            def group_sum(L, r, u, s):
                A = AS[L]
                pe.wait_ge(A["onehot"], r * NG + S1 * u + s + 1)
                pe.wait_ge(A["gathered"][s], 16 * J * (r * (NG // S1) + u + 1))
                for j in range(J):
                    last = nc.tensor.matmul(ps[:, s, 0:WIN], rows_g[:, s, j, :], onehot[:, s, j, 0:WIN],
                                            start=j == 0, stop=j == J - 1)
                if L == 0:
                    for j in range(J):
                        last = nc.tensor.matmul(ps[:, s, WIN:2 * WIN], ones[:, :], onehot[:, s, j, 0:WIN],
                                                start=j == 0, stop=j == J - 1)
                last.then_inc(A["psum"], 1)

            def bucket_offsets(r, b, s):
                pe.wait_ge(q_scan, r * (NB + 1) + b + 1)
                total = counts[s][:, NTILE - 1:NTILE]
                nc.tensor.matmul(ps[:, 4 + s, 0:1], upper[:, :], total, start=True, stop=True)
                nc.tensor.matmul(ps[:, 4 + s, 1:2], ones[:, :], total, start=True, stop=True).then_inc(q_off, 1)

            def move_edges(tile, j):
                pe.wait_ge(q_hot, tile + 1)
                for c in range(2):
                    for h in range(2):
                        last = nc.tensor.matmul(ps[:, 4 + 2 * c + h, 0:HT], hot_l[:, j, c, :],
                                                hot_h[:, j, h * HT:(h + 1) * HT], start=False, stop=False)
                last.then_inc(q_moved, 1)

            def all_places(first):
                for b in range(4):
                    last = nc.tensor.matmul(ps[:, 4 + b, 0:HT], nought[:, 0:P], nought[:, :],
                                            start=first, stop=not first)
                return last

            for L in range(2):
                A = AS[L]
                if L == 1:
                    pe.wait_ge(LS[0]["rows"], NC)
                    pe.wait_ge(LS[0]["kept"], NC)

                def own_product(c, s):
                    for h in range(2):
                        last = nc.tensor.matmul(ps[:, 4 + 2 * s + h, 0:HALF], wr[L][:, :],
                                                hT[:, bass.ds(c * CW + h * HALF, HALF)], start=True, stop=True)
                    last.then_inc(LS[L]["own"], 1)

                for s in range(2):
                    own_product(s, s)
                with pe.Fori(1, NC // 2) as u:
                    for s in range(2):
                        pe.wait_ge(LS[L]["own_ok"], 2 * u + s - 1)
                        own_product(2 * u + s, s)
                pe.wait_ge(LS[L]["own_ok"], NC)
                if L == 1:
                    pe.sem_inc(q_moved, J)
                with pe.Fori(0, rounds) as r:
                    if L == 1:
                        all_places(True)
                    with pe.Fori(0, NG // S1 - 1) as u:
                        for s in range(S1):
                            group_sum(L, r, u, s)
                            if L == 0 and s % 2:
                                bucket_offsets(r, 2 * u + s // 2, s // 2)
                            if L == 1:
                                for j in range(J):
                                    move_edges(r * NTILE + J * (S1 * u + s) + j, j)
                    for s in range(S1):
                        group_sum(L, r, NG // S1 - 1, s)
                        if L == 1:
                            for j in range(J):
                                move_edges(r * NTILE + NTILE - J * (S1 - s) + j, j)
                    if L == 1:
                        all_places(False).then_inc(q_placed, 1)

                def linear(c, s):
                    pe.wait_ge(LS[L]["relu"], c + 1)
                    for k in range(CT):
                        o = 1024 * s + k * P
                        columns = tslot[:, s, k * P:(k + 1) * P]
                        if L == 0:
                            last = nc.tensor.matmul(ps_f[:, o:o + P], columns, wl[1][:, :], start=True, stop=True)
                        else:
                            last = nc.tensor.transpose(ps_f[:, o:o + P], columns, ident[:, :])
                    last.then_inc(LS[L]["tr"], 1)

                for s in range(2):
                    linear(s, s)
                with pe.Fori(1, NC // 2) as u:
                    for s in range(2):
                        pe.wait_ge(LS[L]["rows"], 2 * u + s - 1)
                        linear(2 * u + s, s)

            def ab_products(c, s, first=False):
                pe.wait_ge(NS[1]["t_ok"], c + 1)
                for h, (done, read) in enumerate((("a_ps", "a_ok"), ("b_ps", "b_ok"))):
                    if not first:
                        pe.wait_ge(NS[1][read], c)
                    for k in range(CT):
                        o = 2048 + 1024 * h + k * D
                        last = nc.tensor.matmul(ps_f[:, o:o + D], tslot[:, s, k * P:(k + 1) * P],
                                                w_ab[:, h * D:(h + 1) * D], start=True, stop=True)
                    last.then_inc(NS[1][done], 1)

            for s in range(2):
                norm_transpose(NS[1], s, s)
            for s in range(2):
                ab_products(s, s, s == 0)
                norm_transpose(NS[1], 2 + s, s)
            with pe.Fori(1, NC // 2 - 1) as u:
                for s in range(2):
                    ab_products(2 * u + s, s)
                    norm_transpose(NS[1], 2 * u + 2 + s, s)
            for s in range(2):
                ab_products(NC - 2 + s, s)
            pe.wait_ge(NS[1]["a_ok"], NC)
            pe.wait_ge(NS[1]["b_ok"], NC)

            pe.sem_inc(e_sum, 2)
            pe.wait_ge(e_rounds, 1)
            rounds = pe.value_load(rounds_e[0:1, 0:1], min_val=1, max_val=MAXR)
            A = AS[2]

            def turn(it, s):
                pe.wait_ge(A["onehot"], it + 1)
                for j in range(J):
                    last = nc.tensor.transpose(ps[:, s % 2, j * P:(j + 1) * P], onehot[:, s, j, :], ident[:, :])
                last.then_inc(e_turned, 1)

            def edge_sum(r, it, k, s):
                pe.wait_ge(e_ohT, it + 1)
                pe.wait_ge(e_awin[s % 2], 16 * (r * (NG // 2) + 2 * k + s // 2 + 1))
                pe.wait_ge(A["gathered"][s], 16 * J * (r * (NG // S1) + k + 1))
                for j in range(J):
                    nc.tensor.matmul(ps[:, 2 + s % 2, j * D:(j + 1) * D], ohT[:, s % 2, j * P:(j + 1) * P],
                                     awin[:, s % 2, :], start=True, stop=False)
                    last = nc.tensor.matmul(ps[:, 2 + s % 2, j * D:(j + 1) * D], ident[:, :], rows_g[:, s, j, :],
                                            start=False, stop=True)
                last.then_inc(e_sum, 1)

            def source_sum(it, s):
                pe.wait_ge(e_msg, it + 1)
                for j in range(J):
                    last = nc.tensor.matmul(ps[:, 4 + s % 2, 0:WIN3], msg[:, s % 2, j, :], onehot[:, s, j, :],
                                            start=j == 0, stop=j == J - 1)
                last.then_inc(A["psum"], 1)

            with pe.Fori(0, rounds) as r:
                turn(r * NG, 0)
                turn(r * NG + 1, 1)
                edge_sum(r, r * NG, 0, 0)
                with pe.Fori(0, NG // S1 - 1) as u:
                    for s in range(S1):
                        it = r * NG + S1 * u + s
                        turn(it + 2, (s + 2) % S1)
                        source_sum(it, s)
                        edge_sum(r, it + 1, u + (s + 1) // S1, (s + 1) % S1)
                for s in range(S1):
                    it = r * NG + NG - S1 + s
                    if s + 2 < S1:
                        turn(it + 2, s + 2)
                    else:
                        pe.wait_ge(A["added"], it)
                    source_sum(it, s)
                    if s + 1 < S1:
                        edge_sum(r, it + 1, NG // S1 - 1, s + 1)

            def update(c, s):
                pe.wait_ge(o_y, c + 1)
                for k in range(CT):
                    o = 2048 * s + k * P
                    last = nc.tensor.matmul(ps_f[:, o:o + P], tslot[:, s, k * P:(k + 1) * P], w_u[:, :],
                                            start=True, stop=True)
                last.then_inc(o_lin, 1)

            for s in range(2):
                update(s, s)
            with pe.Fori(1, NC // 2) as u:
                for s in range(2):
                    pe.wait_ge(o_biased, 2 * u + s - 1)
                    update(2 * u + s, s)

        @block.vector
        def _(dve):
            steps = [0]

            def link(instruction):
                steps[0] += 1
                instruction.then_inc(s_dve, 1)
                dve.wait_ge(s_dve, steps[0])

            v = nc.vector
            dve.wait_ge(s_edges, 16 * 6)
            dve.wait_ge(s_const, 7)
            v.tensor_copy(dst_rf, dst_r)
            link(v.tensor_copy(src_rf, src_r))
            link(v.tensor_reduce(out=gmin[:, :], in_=dst_rf, op=ALU.min, axis=AX.X))
            link(v.tensor_reduce(out=gspan[:, :], in_=dst_rf, op=ALU.max, axis=AX.X))
            link(v.tensor_tensor(out=gspan[:, :], in0=gspan[:, :], in1=gmin[:, :], op=ALU.subtract))
            for h in range(2):
                v.tensor_scalar(diag[:, h, :], ident[0:HG, 0:HG], gmin[:, h:h + 1], None, ALU.mult
                                ).then_inc(s_diag, 1)
                v.tensor_scalar(diag[:, 2 + h, :], ident[0:HG, 0:HG], gspan[:, h:h + 1], None, ALU.mult
                                ).then_inc(s_diag, 1)
            def tile_stats(t):
                return v.bn_stats(stats[:, bass.ds(t, 1), :].rearrange("p a k -> p (a k)"),
                                  x_sb[:, bass.ds(t, 1), :].rearrange("p a f -> p (a f)"))

            def x_stats(part, t0, t1):
                dve.wait_ge(s_x[part], 16 * (part + 1))
                with dve.Fori(t0 // (2 * CT), t1 // (2 * CT)) as u:
                    for k in range(2 * CT):
                        last = tile_stats(2 * CT * u + k)
                    last.then_inc(NS[0]["bnst"], 1)

            x_stats(0, 0, X_EARLY)
            dve.wait_ge(s_et, 1)
            for h in range(2):
                for a, to in enumerate((dst_f, src_i)):
                    v.tensor_copy(to[:, h * HG:(h + 1) * HG, :].rearrange("p g j -> p j g"),
                                  ps[:, 2 * h + a, 0:J * HG].rearrange("p (j g) -> p j g", j=J))
            v.tensor_copy(base_f[:, :], ps[:, 4, 0:NG])
            link(v.tensor_reduce(out=span[:, :], in_=ps[0:1, 5, 0:NG], op=ALU.max, axis=AX.X))
            def count_rounds(to, ready):
                link(v.tensor_scalar(reached[:, :], thr[:, :], span[:, 0:1], None, ALU.is_le))
                link(v.tensor_reduce(out=rounds_f[:, :], in_=reached[:, :], op=ALU.add, axis=AX.X))
                v.tensor_scalar(to[:, :], rounds_f[:, :], 1.0, None, ALU.add).then_inc(ready, 1)

            count_rounds(rounds_i, s_rounds)

            def norm_stats(S):
                def st(k):
                    return stats[:, :, k:k + 1].rearrange("p t a -> p (t a)")

                def w(k):
                    return lnw[:, k, :]
                v.tensor_tensor(out=w(0), in0=st(1), in1=st(4), op=ALU.add)
                v.tensor_tensor(out=w(1), in0=st(1), in1=st(4), op=ALU.subtract)
                link(v.tensor_tensor(out=w(2), in0=st(2), in1=st(5), op=ALU.add))
                v.tensor_scalar(w(0), w(0), 0.5, None, ALU.mult)
                v.tensor_scalar(w(2), w(2), 1.0 / D, EPS, ALU.mult, ALU.add)
                link(v.scalar_tensor_tensor(out=w(1), in0=w(1), scalar=0.25, in1=w(1), op0=ALU.mult, op1=ALU.mult))
                v.tensor_tensor(out=w(3), in0=w(2), in1=w(1), op=ALU.add).then_inc(S["var"], 1)
                dve.wait_ge(S["sqrt"], 1)
                link(v.reciprocal(w(7), w(4)))
                link(v.tensor_tensor(out=w(7), in0=w(7), in1=w(3), op=ALU.mult))
                link(v.tensor_tensor(out=w(7), in0=w(7), in1=w(4), op=ALU.add))
                link(v.tensor_scalar(w(7), w(7), 0.5, None, ALU.mult))
                link(v.reciprocal(w(5), w(7)))
                v.scalar_tensor_tensor(out=w(6), in0=w(0), scalar=-1.0, in1=w(5), op0=ALU.mult, op1=ALU.mult
                                       ).then_inc(S["ln"], 1)

            def window_steps(A, win):
                def first():
                    v.tensor_copy(base_w[:, :], base_f[0:1, :])
                    link(v.tensor_tensor(out=rel_f[:, :, :], in0=dst_f[:, :, :],
                                         in1=base_f[:, :].unsqueeze(2).to_broadcast([P, NG, J]), op=ALU.subtract))
                    v.tensor_scalar(base_i[:, :], base_w[:, :], float(ROWS - win), None, ALU.min
                                    ).then_inc(A["window"], 1)

                def following(r):
                    dve.wait_ge(A["added"], r * NG + NG + 1)
                    dve.wait_ge(A["onehot"], r * NG + NG)
                    v.tensor_scalar(base_w[:, :], base_w[:, :], float(win), None, ALU.add).then_inc(A["shift"], 1)
                    v.tensor_scalar(rel_f[:, :, :], rel_f[:, :, :], float(-win), None, ALU.add
                                    ).then_inc(A["shift"], 1)
                    dve.wait_ge(A["shift"], 2 * r + 2)
                    v.tensor_scalar(base_i[:, :], base_w[:, :], float(ROWS - win), None, ALU.min
                                    ).then_inc(A["window"], 1)
                return first, following

            dve.wait_ge(s_rounds, 1)
            rounds = dve.value_load(rounds_i[0:1, 0:1], min_val=1, max_val=MAXR)
            first, following = window_steps(AS[0], WIN)
            first()
            x_stats(1, X_EARLY, NT)
            dve.wait_ge(NS[0]["bnst"], NC // 2)
            norm_stats(NS[0])

            def keep_T(c, s):
                dve.wait_ge(NS[0]["hT_ps"], c + 1)
                v.tensor_copy(tslot[:, s, :], ps_f[:, 1024 * s:1024 * s + CW]).then_inc(NS[0]["t_ok"], 1)
                dve.wait_ge(NS[0]["t_ok"], c + 1)
                v.tensor_copy(hT[:, bass.ds(c * CW, CW)], tslot[:, s, :]).then_inc(NS[0]["kept"], 1)

            def keep_rows(c, s):
                dve.wait_ge(NS[0]["product"], c + 1)
                v.tensor_copy(mslot[:, s, :], ps_f[:, 2048 + 1024 * s:2048 + 1024 * s + CW]
                              ).then_inc(NS[0]["rows"], 1)

            for s in range(2):
                keep_T(s, s)
            for s in range(2):
                keep_rows(s, s)
                dve.wait_ge(NS[0]["kept"], s + 1)
                keep_T(2 + s, s)
            with dve.Fori(1, NC // 2 - 1) as u:
                for s in range(2):
                    dve.wait_ge(NS[0]["st"][s], 16 * u)
                    keep_rows(2 * u + s, s)
                    dve.wait_ge(NS[0]["kept"], 2 * u + s + 1)
                    keep_T(2 * u + 2 + s, s)
            for s in range(2):
                dve.wait_ge(NS[0]["st"][s], 16 * (NC // 2 - 1))
                keep_rows(NC - 2 + s, s)


            def group_steps(A, win, halves, bank, with_indices=False):
                def prepare(g, s):
                    if with_indices:
                        v.tensor_copy(idx1[:, s, :], src_i[:, bass.ds(g, 1), :].rearrange("p a j -> p (a j)")
                                      ).then_inc(A["idx"], 1)
                    v.tensor_tensor(out=onehot[:, s, :, 0:win],
                                    in0=iota_w[:, 0:win].unsqueeze(1).to_broadcast([P, J, win]),
                                    in1=rel_f[:, bass.ds(g, 1), :].rearrange("p a j -> p j a").to_broadcast(
                                        [P, J, win]), op=ALU.is_equal).then_inc(A["onehot"], 1)

                def add(r, g, s):
                    base = dve.value_load(base_i[0:1, bass.ds(g, 1)], min_val=0, max_val=ROWS - win)
                    dve.wait_ge(A["psum"], r * NG + g + 1)
                    dve.wait_ge(A["added"], r * NG + g + 1)
                    v.tensor_tensor(out=agg[:, 0:halves, bass.ds(base, win)],
                                    in0=agg[:, 0:halves, bass.ds(base, win)],
                                    in1=ps[:, bank(s), 0:halves * win].rearrange("p (h w) -> p h w", h=halves),
                                    op=ALU.add).then_inc(A["added"], 1)
                return prepare, add

            def chained(semaphore, base):
                n = [0]

                def chain(instruction):
                    n[0] += 1
                    instruction.then_inc(semaphore, 1)
                    dve.wait_ge(semaphore, base + n[0])
                return chain, n

            SETUP, STEP = 11, 4

            def places_setup(r):
                chain, n = chained(q_setup, r * SETUP)
                v.memset(place[:, :], 0.0)
                v.memset(bucket[:, :], -1.0)
                v.memset(bfirst[:, 0:NG], -1.0)
                chain(v.memset(starts[:, 0:1], 0.0))
                chain(v.tensor_scalar(ints, src_l, BUCK.bit_length() - 1, None, ALU.arith_shift_right))
                chain(v.tensor_copy(src_b[:, :], ints))
                chain(v.tensor_scalar(ints, src_l, BUCK - 1, None, ALU.bitwise_and))
                chain(v.tensor_scalar(carry1[:, :], ints, 4.0, None, ALU.mult))
                chain(v.tensor_copy(here.bitcast(i32), dst_l))
                chain(v.tensor_scalar(ints, here.bitcast(i32), LOW - 1, None, ALU.bitwise_and))
                chain(v.tensor_copy(carry0[:, :], ints))
                chain(v.tensor_scalar(ints, here.bitcast(i32), LOW.bit_length() - 1, None, ALU.arith_shift_right))
                chain(v.tensor_copy(here, ints))
                chain(v.tensor_tensor(out=carry1[:, :], in0=carry1[:, :], in1=here, op=ALU.add))
                assert n[0] == SETUP
                nc.vector.sem_inc(q_past, 1)

            def count_bucket(r, b, slot, base, k):
                v.tensor_scalar(heres[slot], src_b[:, :], bnum[:, bass.ds(b, 1)], None, ALU.is_equal
                                ).then_inc(q_step, 1)
                dve.wait_ge(q_step, base + k + 1)
                v.tensor_tensor_scan(counts[slot], ones[:, 0:1].to_broadcast([P, NTILE]), heres[slot], 0.0,
                                     ALU.mult, ALU.add).then_inc(q_scan, 1)

            def place_bucket(r, b, slot):
                base = r * (1 + STEP * NB) + 1 + STEP * b
                start = starts[:, bass.ds(b, 1)]
                here, count = heres[slot], counts[slot]
                dve.wait_ge(q_off, r * NB + b + 1)
                v.tensor_scalar(offset[:, :], ps[:, 4 + slot, 0:1], start, -1.0, ALU.add, ALU.add)
                v.tensor_scalar(starts[:, bass.ds(b + 1, 1)], ps[:, 4 + slot, 1:2], start, None, ALU.add
                                ).then_inc(q_step, 1)
                v.scalar_tensor_tensor(out=bfirst[:, 0:NG], in0=gnum[:, :], scalar=start, in1=bfirst[:, 0:NG],
                                       op0=ALU.is_ge, op1=ALU.add)
                dve.wait_ge(q_step, base + 1)
                v.scalar_tensor_tensor(out=count, in0=count, scalar=offset[:, 0:1], in1=here,
                                       op0=ALU.add, op1=ALU.mult).then_inc(q_step, 1)
                v.scalar_tensor_tensor(out=bucket[:, :], in0=pnum, scalar=start, in1=bucket[:, :],
                                       op0=ALU.is_ge, op1=ALU.add)
                dve.wait_ge(q_step, base + 2)
                v.tensor_tensor(out=place[:, :], in0=place[:, :], in1=count, op=ALU.add).then_inc(q_step, 1)
                count_bucket(r, b + 1, 1 - slot, base, 3)

            def hot_places(r, g):
                for j in range(J):
                    tile = J * g + j
                    dve.wait_ge(q_moved, r * NTILE + tile + 1)
                    v.tensor_scalar(hot_h[:, j, :], iota_h[:, :], src_b[:, bass.ds(tile, 1)], None, ALU.is_equal)
                    v.tensor_scalar(hot_l[:, j, 0, :], iota_l[:, :], place[:, bass.ds(tile, 1)],
                                    carry0[:, bass.ds(tile, 1)], ALU.is_equal, ALU.mult)
                    v.tensor_scalar(hot_l[:, j, 1, :], iota_l[:, :], place[:, bass.ds(tile, 1)],
                                    carry1[:, bass.ds(tile, 1)], ALU.is_equal, ALU.mult).then_inc(q_hot, 1)

            for L in range(2):
                A = AS[L]
                halves = 2 if L == 0 else 1
                prepare, add = group_steps(A, WIN, halves, lambda s: s)
                if L == 1:
                    link(v.tensor_copy(ints, place[:, :]))
                    link(v.tensor_scalar(here.bitcast(i32), ints, P.bit_length() - 1, None, ALU.arith_shift_right))
                    v.tensor_copy(src_b[:, :], here.bitcast(i32))
                    link(v.tensor_scalar(ints, ints, P - 1, None, ALU.bitwise_and))
                    link(v.tensor_copy(place[:, :], ints))
                with dve.Fori(0, rounds) as r:
                    dve.wait_ge(A["window"], r + 1)
                    for s in range(S1):
                        prepare(s, s)
                    if L == 0:
                        dve.wait_ge(s_order, 6)
                        places_setup(r)
                        count_bucket(r, 0, 0, r * (1 + STEP * NB), 0)
                    with dve.Fori(0, NG // S1 - 1) as u:
                        for s in range(S1):
                            if L == 1:
                                hot_places(r, S1 * u + s)
                            add(r, S1 * u + s, s)
                            prepare(S1 * u + S1 + s, s)
                            if L == 0 and s % 2:
                                place_bucket(r, 2 * u + s // 2, s // 2)
                    for s in range(S1):
                        if L == 1:
                            hot_places(r, NG - S1 + s)
                        add(r, NG - S1 + s, s)
                    if L == 0:
                        dve.wait_ge(q_scan, (r + 1) * (NB + 1))
                    following(r)
                dve.wait_ge(A["added"], rounds * NG + 1)
                def total(u, s, count=None, used=True):
                    c = 2 * u + s
                    if s and L == 0:
                        if used:
                            dve.wait_ge(LS[L]["sum"][s], u)
                        v.tensor_tensor(out=pslot[:, s, :], in0=agg[:, 0, bass.ds(c * CW, CW)],
                                        in1=agg[:, 1, bass.ds(c * CW, CW)] if count is None else count,
                                        op=ALU.mult).then_inc(LS[L]["odd"], 1)
                        dve.wait_ge(LS[L]["odd"], u + 1)
                    elif s:
                        return
                    else:
                        dve.wait_ge(LS[L]["mean"], u + 1)
                    if used:
                        dve.wait_ge(LS[L]["kept" if L == 0 else "relu"], c - 1)
                    v.tensor_tensor(out=mslot[:, s, :], in0=pslot[:, s, :], in1=hT[:, bass.ds(c * CW, CW)],
                                    op=ALU.add).then_inc(LS[L]["sum"][s], 1)

                def finish(c, s):
                    dve.wait_ge(LS[L]["tr"], c + 1)
                    rows = ps_f[:, 1024 * s:1024 * s + CW].rearrange("p (t f) -> p t f", f=D)
                    if L == 0:
                        v.tensor_copy(hrow[:, s, :, :], rows).then_inc(LS[L]["rows"], 1)
                    else:
                        xs = x_sb[:, bass.ds(c * CT, CT), :]
                        v.tensor_tensor(out=xs, in0=xs, in1=rows, op=ALU.add).then_inc(LS[L]["rows"], 1)
                        dve.wait_ge(LS[L]["rows"], c + 1)
                        for k in range(CT):
                            last = tile_stats(c * CT + k)
                        last.then_inc(NS[1]["bnst"], 1)

                def first_reciprocals(c):
                    link(v.tensor_scalar(tslot[:, c, :], agg[:, 1, c * CW:(c + 1) * CW], 1.0, None, ALU.max))
                    v.reciprocal(tslot[:, c, :], tslot[:, c, :]).then_inc(s_first, 1)

                nc.vector.sem_inc(A["done"], 1)
                dve.wait_ge(LS[L]["own_ok"], NC)
                if L == 0:
                    first_reciprocals(0)
                    dve.wait_ge(s_cnt, 16)
                    link(v.tensor_scalar(cnt_cols[:, :], cnt_cols[:, :], 1.0, None, ALU.max))
                    v.reciprocal(cnt_cols[:, :], cnt_cols[:, :]).then_inc(s_rcnt, 1)
                    total(0, 0, used=False)
                    first_reciprocals(1)
                    dve.wait_ge(s_first, 2)
                    total(0, 1, tslot[:, 1, :], used=False)
                    total(1, 0)
                    finish(0, 0)
                    dve.wait_ge(s_spread[0], 16)
                    total(1, 1)
                    finish(1, 1)
                    first, following = window_steps(AS[1], WIN)
                    first()
                    dve.wait_ge(s_spread[1], 16)
                else:
                    dve.wait_ge(q_carried, 2)
                    v.tensor_scalar(here.bitcast(i32), carry1[:, :].bitcast(i32), 3, None, ALU.bitwise_and
                                    ).then_inc(q_cut, 1)
                    total(0, 0, used=False)
                    v.tensor_scalar(ints, carry1[:, :].bitcast(i32), 2, None, ALU.arith_shift_right
                                    ).then_inc(q_cut, 1)
                    total(1, 0)
                    finish(0, 0)
                    dve.wait_ge(q_carried, 4)
                    dve.wait_ge(A["idx"], rounds * NG + S1)
                    v.scalar_tensor_tensor(out=src_l, in0=pnum, scalar=float(LOW), in1=carry0[:, :],
                                           op0=ALU.mult, op1=ALU.add)
                    finish(1, 1)
                    dve.wait_ge(q_carried, 5)
                    v.scalar_tensor_tensor(out=dst_l, in0=bucket[:, :], scalar=float(BUCK), in1=gone,
                                           op0=ALU.mult, op1=ALU.add).then_inc(q_sorted, 1)
                with dve.Fori(1, NC // 2 - 1) as u:
                    for s in range(2):
                        total(u + 1, s)
                        if L == 0:
                            dve.wait_ge(LS[L]["st"][s], 16 * u)
                        finish(2 * u + s, s)
                for s in range(2):
                    if L == 0:
                        dve.wait_ge(LS[L]["st"][s], 16 * (NC // 2 - 1))
                    finish(NC - 2 + s, s)

            dve.wait_ge(NS[1]["bnst"], NC)
            norm_stats(NS[1])
            v.memset(bfirst[:, NG:NG + 1], float(PAD // BUCK))
            link(v.tensor_scalar(base_f[:, :], bfirst[:, 0:NG], float(BUCK), None, ALU.mult))
            link(v.tensor_tensor(out=width[:, :], in0=bfirst[0:1, 1:NG + 1], in1=bfirst[0:1, 0:NG],
                                 op=ALU.subtract))
            link(v.tensor_reduce(out=span[:, :], in_=width[:, :], op=ALU.max, axis=AX.X))
            link(v.tensor_scalar(span[:, :], span[:, :], float(BUCK * WIN // WIN3), None, ALU.mult))
            count_rounds(rounds_e, e_rounds)
            dve.wait_ge(q_sorted, 1)
            A = AS[2]
            first, following = window_steps(A, WIN3)
            prepare, add = group_steps(A, WIN3, 1, lambda s: 4 + s % 2, True)
            first()

            def keep_h3(c, s):
                dve.wait_ge(NS[1]["hrows"], c + 1)
                xs = x_sb[:, bass.ds(c * CT, CT), :]
                v.tensor_tensor(out=xs, in0=xs, in1=hrow[:, s, :, :], op=ALU.add).then_inc(NS[1]["hT_ok"], 1)
                dve.wait_ge(NS[1]["hT_ps"], c + 1)
                v.tensor_copy(tslot[:, s, :], ps_f[:, 1024 * s:1024 * s + CW]).then_inc(NS[1]["t_ok"], 1)

            def b_part(c, s):
                dve.wait_ge(NS[1]["b_ps"], c + 1)
                v.tensor_tensor(out=abslot[:, s, :, D:2 * D],
                                in0=ps_f[:, 3072:3072 + CW].rearrange("p (t f) -> p t f", f=D),
                                in1=bias[:, 0:1, :].to_broadcast([P, CT, D]), op=ALU.add).then_inc(NS[1]["b_ok"], 1)

            for s in range(2):
                keep_h3(s, s)
            for s in range(2):
                b_part(s, s)
                dve.wait_ge(NS[1]["kept"], s + 1)
                keep_h3(2 + s, s)
            with dve.Fori(1, NC // 2 - 1) as u:
                for s in range(2):
                    dve.wait_ge(NS[1]["st_b"][s], 16 * u)
                    b_part(2 * u + s, s)
                    dve.wait_ge(NS[1]["kept"], 2 * u + s + 1)
                    keep_h3(2 * u + 2 + s, s)
            for s in range(2):
                dve.wait_ge(NS[1]["st_b"][s], 16 * (NC // 2 - 1))
                b_part(NC - 2 + s, s)

            dve.wait_ge(e_rounds, 1)
            rounds = dve.value_load(rounds_e[0:1, 0:1], min_val=1, max_val=MAXR)
            dve.wait_ge(NS[1]["kept"], NC)
            nc.vector.sem_inc(A["added"], 1)
            with dve.Fori(0, rounds) as r:
                dve.wait_ge(A["window"], r + 1)
                for s in range(S1):
                    prepare(s, s)
                with dve.Fori(0, NG // S1 - 1) as u:
                    for s in range(S1):
                        add(r, S1 * u + s, s)
                        prepare(S1 * u + S1 + s, s)
                for s in range(S1):
                    add(r, NG - S1 + s, s)
                following(r)
            dve.wait_ge(A["added"], rounds * NG + 1)
            nc.vector.sem_inc(e_done, 1)

            def biased(c, s):
                dve.wait_ge(o_lin, c + 1)
                v.tensor_tensor(out=hrow[:, s, :, :],
                                in0=ps_f[:, 2048 * s:2048 * s + CW].rearrange("p (t f) -> p t f", f=D),
                                in1=bias[:, 1:2, :].to_broadcast([P, CT, D]), op=ALU.add).then_inc(o_biased, 1)

            def residual(c, s):
                dve.wait_ge(o_biased, c + 1)
                xs = x_sb[:, bass.ds(c * CT, CT), :]
                v.scalar_tensor_tensor(out=xs, in0=hrow[:, s, :, :], scalar=0.0, in1=xs, op0=ALU.max, op1=ALU.add
                                       ).then_inc(o_sum, 1)

            biased(0, 0)
            biased(1, 1)
            residual(0, 0)
            with dve.Fori(1, NC // 2) as u:
                for s in range(2):
                    dve.wait_ge(o_sum, 2 * u + s - 1)
                    biased(2 * u + s, s)
                    residual(2 * u + s - 1, 1 - s)
            residual(NC - 1, 1)


_INS = ['x', 'src', 'dst', 'L0_gnn_W_l0', 'L0_gnn_W_r0', 'L0_gnn_b0', 'L0_gnn_W_l1', 'L0_gnn_W_r1', 'L0_gnn_b1',
        'L1_gnn_W_interact', 'L1_gnn_b_interact', 'L1_gnn_W_update', 'L1_gnn_b_update']


def kernel(**inputs):
    import numpy as _np
    import concourse.bacc as _bacc
    from concourse import mybir as _mybir
    from concourse.bass_utils import run_bass_kernel_spmd as _run

    nc = _bacc.Bacc("TRN2", target_bir_lowering=False, num_devices=1)
    arrays, args = {}, []
    for name in _INS:
        a = _np.ascontiguousarray(inputs[name])
        arrays[f"in_{name}"] = a
        args.append(nc.dram_tensor(f"in_{name}", a.shape, _mybir.dt.from_np(a.dtype), kind="ExternalInput").ap())
    out = nc.dram_tensor("out_0", inputs['x'].shape, _mybir.dt.float32, kind="ExternalOutput").ap()
    gnn_kernel(nc, *args, out)
    r = _run(nc, [arrays], core_ids=[0])
    return r.results[0]["out_0"]
```
